# Optimizing a Trainium2 kernel written in Bass

```python
import numpy as np
import jax
import jax.numpy as jnp

def _softmax(x, axis=-1):
    return jax.nn.softmax(x, axis=axis)

def _gelu(x):
    return jax.nn.gelu(x, approximate=True)

def _silu(x):
    return jax.nn.silu(x)

def _sigmoid(x):
    return jax.nn.sigmoid(x)

def _layernorm(x, axis=-1, eps=1e-05):
    m = jnp.mean(x, axis=axis, keepdims=True)
    v = jnp.var(x, axis=axis, keepdims=True)
    return (x - m) / jnp.sqrt(v + eps)

def _scatter_add(tgt, idx, src, axis=0):
    return tgt.at[idx].add(src)

def _segment_sum(src, seg, n):
    return jax.ops.segment_sum(src, seg, n)
kernel_name = 'mk_macaron_d1_jaxref_r8_d8ef2b'

def setup_inputs(seed: int=0):
    np.random.seed(seed)
    _w = jnp.asarray

    def _L0_attn_setup():
        import jax, jax.numpy as jnp
        import numpy as np
        D_MODEL = 128
        N_HEADS = 16
        D_HEAD = D_MODEL // N_HEADS
        BATCH = 2
        SEQ = 256
        key = jax.random.key(seed)
        ks = jax.random.split(key, 5)
        s = 1.0 / np.sqrt(D_MODEL)
        return {'x': jax.random.normal(ks[0], (BATCH, SEQ, D_MODEL), dtype=jnp.float32), 'W_qkv': jax.random.normal(ks[1], (3 * D_MODEL, D_MODEL), dtype=jnp.float32) * s, 'b_qkv': jax.random.normal(ks[2], (3 * D_MODEL,), dtype=jnp.float32) * 0.01, 'W_out': jax.random.normal(ks[3], (D_MODEL, D_MODEL), dtype=jnp.float32) * s, 'b_out': jax.random.normal(ks[4], (D_MODEL,), dtype=jnp.float32) * 0.01}
    _L0_attn_in = _L0_attn_setup()

    def _L0_ffn_setup():
        import jax, jax.numpy as jnp
        import numpy as np
        B, S, D = (2, 256, 128)
        H, E, P, K = (8, 8, 128, 2)
        SCALE = 1.0 / np.sqrt(P)

        def _get_sel_gate(x, w, route_scale):
            logits = jnp.einsum('bsd,ed->bse', x, w).astype(jnp.float32)
            raw = logits.reshape(x.shape[0], x.shape[1], H, E)
            probs = jax.nn.sigmoid(raw)
            vals, idx = jax.lax.top_k(probs, K)
            vals = vals / jnp.clip(vals.sum(-1, keepdims=True), 1e-09)
            vals = vals * route_scale
            gate = (jax.nn.one_hot(idx, E, dtype=vals.dtype) * vals[..., None]).sum(-2)
            return gate
        key = jax.random.key(seed)
        ks = jax.random.split(key, 8)
        std = 1.0 / np.sqrt(D)
        return {'x': jax.random.normal(ks[0], (B, S, D), jnp.float32), 'q_w': jax.random.normal(ks[1], (H * P, D), jnp.float32) * std, 'k_w': jax.random.normal(ks[2], (H * P, D), jnp.float32) * std, 'v_w': jax.random.normal(ks[3], (H * E, D, P), jnp.float32) * std, 'o_w': jax.random.normal(ks[4], (H * E, P, D), jnp.float32) * (1.0 / np.sqrt(H * P)), 'sel_v_w': jax.random.normal(ks[5], (H * E, D), jnp.float32) * std, 'sel_o_w': jax.random.normal(ks[6], (H * E, D), jnp.float32) * std, 'route_scale': jnp.ones((1,), jnp.float32)}
    _L0_ffn_in = _L0_ffn_setup()
    _d = {'L0_attn_x': _L0_attn_in['x'], 'L0_attn_W_qkv': _L0_attn_in['W_qkv'], 'L0_attn_b_qkv': _L0_attn_in['b_qkv'], 'L0_attn_W_out': _L0_attn_in['W_out'], 'L0_attn_b_out': _L0_attn_in['b_out'], 'L0_ffn_q_w': _L0_ffn_in['q_w'], 'L0_ffn_k_w': _L0_ffn_in['k_w'], 'L0_ffn_v_w': _L0_ffn_in['v_w'], 'L0_ffn_o_w': _L0_ffn_in['o_w'], 'L0_ffn_sel_v_w': _L0_ffn_in['sel_v_w'], 'L0_ffn_sel_o_w': _L0_ffn_in['sel_o_w'], 'L0_ffn_route_scale': _L0_ffn_in['route_scale']}
    _x0 = _d['L0_attn_x']
    _d['L0_attn_x'] = jax.random.normal(jax.random.fold_in(jax.random.key(seed), 1), (4, 512, 128), dtype=_x0.dtype)
    del _x0
    return _d

def reference(L0_attn_x, L0_attn_W_qkv, L0_attn_b_qkv, L0_attn_W_out, L0_attn_b_out, L0_ffn_q_w, L0_ffn_k_w, L0_ffn_v_w, L0_ffn_o_w, L0_ffn_sel_v_w, L0_ffn_sel_o_w, L0_ffn_route_scale):

    def _L0_attn_ref(x, W_qkv, b_qkv, W_out, b_out):
        import jax, jax.numpy as jnp
        import numpy as np
        D_MODEL = 128
        N_HEADS = 16
        D_HEAD = D_MODEL // N_HEADS
        BATCH = 2
        SEQ = 256
        b, s, d = x.shape
        qkv = x @ W_qkv.T + b_qkv
        qkv = qkv.reshape(b, s, N_HEADS, 3 * D_HEAD)
        q = qkv[..., :D_HEAD]
        k = qkv[..., D_HEAD:2 * D_HEAD]
        v = qkv[..., 2 * D_HEAD:]
        scale = np.sqrt(D_HEAD).astype(np.float32)
        scores = jnp.einsum('bqhd,bkhd->bhqk', q, k) / scale
        attn = jax.nn.softmax(scores, axis=-1)
        out = jnp.einsum('bhqk,bkhd->bqhd', attn, v)
        out = out.reshape(b, s, d)
        return out @ W_out.T + b_out

    def _L0_ffn_ref(x, q_w, k_w, v_w, o_w, sel_v_w, sel_o_w, route_scale):
        import jax, jax.numpy as jnp
        import numpy as np
        B, S, D = (2, 256, 128)
        H, E, P, K = (8, 8, 128, 2)
        SCALE = 1.0 / np.sqrt(P)

        def _get_sel_gate(x, w, route_scale):
            logits = jnp.einsum('bsd,ed->bse', x, w).astype(jnp.float32)
            raw = logits.reshape(x.shape[0], x.shape[1], H, E)
            probs = jax.nn.sigmoid(raw)
            vals, idx = jax.lax.top_k(probs, K)
            vals = vals / jnp.clip(vals.sum(-1, keepdims=True), 1e-09)
            vals = vals * route_scale
            gate = (jax.nn.one_hot(idx, E, dtype=vals.dtype) * vals[..., None]).sum(-2)
            return gate
        rs = route_scale[0]
        gate_v = _get_sel_gate(x, sel_v_w, rs)
        gate_o = _get_sel_gate(x, sel_o_w, rs)
        q = jnp.einsum('bsd,hpd->bhsp', x, q_w.reshape(H, P, D))
        k = jnp.einsum('bsd,hpd->bhsp', x, k_w.reshape(H, P, D))
        xv = jnp.einsum('bsd,hedp->bshep', x, v_w.reshape(H, E, D, P))
        v = jnp.einsum('bshep,bshe->bhsp', xv, gate_v)
        att = jax.nn.softmax(jnp.einsum('bhqp,bhkp->bhqk', q, k) * SCALE, axis=-1)
        ctx = jnp.einsum('bhqk,bhkp->bqhp', att, v)
        weighted = ctx[:, :, :, None, :] * gate_o[..., None]
        out = jnp.einsum('bshep,hepd->bsd', weighted, o_w.reshape(H, E, P, D))
        return out
    x = L0_attn_x
    x = x + 0.5 * _L0_ffn_ref(_layernorm(x, axis=-1), L0_ffn_q_w, L0_ffn_k_w, L0_ffn_v_w, L0_ffn_o_w, L0_ffn_sel_v_w, L0_ffn_sel_o_w, L0_ffn_route_scale)
    x = x + _L0_attn_ref(_layernorm(x, axis=-1), L0_attn_W_qkv, L0_attn_b_qkv, L0_attn_W_out, L0_attn_b_out)
    x = x + 0.5 * _L0_ffn_ref(_layernorm(x, axis=-1), L0_ffn_q_w, L0_ffn_k_w, L0_ffn_v_w, L0_ffn_o_w, L0_ffn_sel_v_w, L0_ffn_sel_o_w, L0_ffn_route_scale)
    return x

_drawn_inputs = setup_inputs


def setup_inputs(seed=0):
    import zlib

    import numpy as np

    out = dict(_drawn_inputs(seed))
    spreads = {}
    factors = {'L0_attn_b_qkv': 5.929, 'L0_attn_b_out': 5.428}
    for name, (base, spread) in spreads.items():
        noise = np.random.default_rng([zlib.crc32(name.encode()), seed]).standard_normal(out[name].shape)
        drawn = base * np.exp(spread * noise) if base else spread * noise
        out[name] = jnp.asarray(drawn.astype(out[name].dtype))
    for name, factor in factors.items():
        out[name] = (out[name] * factor).astype(out[name].dtype)
    return out
```

```python
from contextlib import ExitStack

import numpy as np
import concourse.bass as bass
from concourse import mybir

F32 = mybir.dt.float32
F32R = mybir.dt.float32r
ALU = mybir.AluOpType
ACT = mybir.ActivationFunctionType
AX = mybir.AxisListType

B, S, D = 4, 512, 128
P = 128
QT = S // P
H, E = 8, 8
HE = H * E
G = 4
NH, DH = 16, 8
NG, GH = 4, 4
R = 32
LN_EPS = 1e-5
FFN_SCALE = 1.0 / float(np.sqrt(P))
MHA_SCALE = 1.0 / float(np.sqrt(DH))
UNITS = H * QT
MU = NG * QT * GH


class Chain:

    def __init__(self, eng, sem):
        self.eng, self.sem, self.done, self.base = eng, sem, 0, 0

    def then(self, ins):
        ins.then_inc(self.sem, 1)
        self.done += 1
        return ins

    def settle(self):
        self.eng.wait_ge(self.sem, self.base + self.done)

    def link(self, ins):
        self.then(ins)
        self.settle()

    def enter(self, i, per):
        self.before, self.per = self.done + 0, per
        self.base, self.done = i * per + self.before, 0

    def leave(self, trips):
        assert self.done == self.per, (self.done, self.per)
        self.base, self.done = 0, self.before + trips * self.per


def macaron_kernel(nc, x, W_qkv, b_qkv, W_out, b_out, q_w, k_w, v_w, o_w, sel_v_w, sel_o_w, route_scale, out):
    ctx = ExitStack()
    with ctx:
        def sb(name, shape, dt=F32, at=ctx):
            return at.enter_context(nc.sbuf_tensor(name, shape, dt))

        def sem(name):
            return ctx.enter_context(nc.semaphore(name))

        xs = sb("xs", [P, B * QT, D])
        wv = sb("wv", [P, 2, HE, P], F32R)
        wo = sb("wo", [P, 2, HE, D], F32R)
        mh = sb("mh", [P, 2, H, D], F32R)
        ident = sb("ident", [P, P])
        selT = sb("selT", [D, 2 * HE])
        wqs = sb("wqs", [D, NG, P])
        wks = sb("wks", [D, NG, P])
        wvT = sb("wvT", [D, NH * DH])
        woT = sb("woT", [NH * DH, D])
        bvb = sb("bvb", [P, NH * DH])
        bout = sb("bout", [1, D])
        bst = sb("bst", [P, 2 * NG + 2])
        ones = sb("ones", [1, P])
        thr = sb("thr", [P, E])
        rsb = sb("rsb", [P, 2 * H])
        ph = sb("ph", [P, QT])
        eps = sb("eps", [P, QT])
        xn = sb("xn", [P, QT, D])
        cnt = sb("cnt", [P, QT * 2 * H, E])
        cmp_ = sb("cmp", [P, QT * 2 * H, E])
        gsum = sb("gsum", [P, QT * 2 * H])
        st = sb("st", [P, QT, 6])
        mv = sb("mv", [P, QT, 2])
        tick = sb("tick", [P, 1])
        ptick = sb("ptick", [P, 1])
        ve = sb("ve", [P, QT])
        rstd = sb("rstd", [P, QT])
        xT = sb("xT", [D, S])
        xhl = sb("xhl", [D, 2, S], F32R)
        gate = sb("gate", [P, QT, 2 * HE])
        gn = sb("gn", [P, 2, QT, E])
        nmin = sb("nmin", [P, 2, QT])
        den = sb("den", [P, 2, QT])
        rden = sb("rden", [P, 2, QT])
        base = ExitStack()
        with base:
            qhl = sb("qhl", [D, 2, S], F32R, base)
            chl = sb("chl", [P, 2, S], F32R, base)
            vv = sb("vv", [P, 2, QT, P], F32, base)
            pt = sb("pt", [P, QT, S], F32, base)
            pp = sb("pp", [P, 2, S], F32, base)
            vt = sb("vt", [P, 2, G * P], F32, base)
            ot = sb("ot", [P, 2, G * D], F32, base)
            acc = sb("acc", [P, QT, G * D], F32, base)
        base = ExitStack()
        with base:
            qk = sb("qk", [P, 2, 2, S], F32R, base)
            vext = sb("vext", [P, QT, NH, R], F32, base)
            pm = sb("pm", [P, GH, S], F32, base)
            ptm = sb("ptm", [P, GH, QT, P], F32, base)
            qkf = sb("qkf", [P, 2, S], F32, base)
            oT = sb("oT", [P, S], F32, base)
            oN = sb("oN", [P, QT, NH, DH], F32, base)
            mmax = sb("mmax", [P, GH], F32, base)
            mrd = sb("mrd", [P, QT, GH], F32, base)
        base = ExitStack()
        with base:
            raw = sb("raw", [P, 4, E, P], F32, base)
            qraw = sb("qraw", [P, H, D], F32, base)
            kraw = sb("kraw", [P, H, D], F32, base)
            wraw = sb("wraw", [P, 3, D], F32, base)
            woraw = sb("woraw", [P, D], F32, base)
            selraw = sb("selraw", [P, D], F32, base)
            braw = sb("braw", [1, 3 * D], F32, base)
            rsraw = sb("rsraw", [1, 1], F32, base)
            brow = sb("brow", [1, 2 * NG + 2, P], F32, base)
            bvrow = sb("bvrow", [1, NH * DH], F32, base)
            mf = sb("mf", [P, H, D], F32, base)

        bank = [ctx.enter_context(nc.psum_tensor(f"bank{i}", [P, 512], F32)) for i in range(8)]
        gb = bank[0:4]
        sbk = bank[4:6]
        tb = bank[6]
        qc = bank[7]

        x_first = sem("x_first")
        x_rest = sem("x_rest")
        small_in = sem("small_in")
        raw_free = sem("raw_free")
        ones_set = sem("ones_set")
        ident_set = sem("ident_set")
        pool_own = sem("pool_own")
        dve_own = sem("dve_own")
        act_own = sem("act_own")
        tr_small = sem("tr_small")
        mh_mm = sem("mh_mm")
        mh_scaled = sem("mh_scaled")
        setup_rows = sem("setup_rows")
        rows_mm = sem("rows_mm")
        sel_ready = sem("sel_ready")
        act_setup = sem("act_setup")
        mv_ready = sem("mv_ready")
        rstd_ready = sem("rstd_ready")
        xn_ready = sem("xn_ready")
        xt_mm = sem("xt_mm")
        xt_ready = sem("xt_ready")
        lg_mm = sem("lg_mm")
        lg_exp = sem("lg_exp")
        prep_done = sem("prep_done")
        q_mm = sem("q_mm")
        q_hi = sem("q_hi")
        q_lo = sem("q_lo")
        s_mm = sem("s_mm")
        s_min = sem("s_min")
        s_exp = sem("s_exp")
        t_mm = sem("t_mm")
        pt_act = sem("pt_act")
        pt_dve = sem("pt_dve")
        av_mm = sem("av_mm")
        c_hi = sem("c_hi")
        c_lo = sem("c_lo")
        gn_ready = sem("gn_ready")
        v0_mm = sem("v0_mm")
        v1_mm = sem("v1_mm")
        o0_mm = sem("o0_mm")
        o1_mm = sem("o1_mm")
        v_act = sem("v_act")
        v_dve = sem("v_dve")
        o_act = sem("o_act")
        o_dve = sem("o_dve")
        v_fold = sem("v_fold")
        o_acc = sem("o_acc")
        x_ffn = sem("x_ffn")
        mv_mm = sem("mv_mm")
        vext_ready = sem("vext_ready")
        qk_mm = sem("qk_mm")
        qkf_ready = sem("qkf_ready")
        qk_ready = sem("qk_ready")
        ms_mm = sem("ms_mm")
        m_max = sem("m_max")
        m_exp = sem("m_exp")
        mt_mm = sem("mt_mm")
        mpt_act = sem("mpt_act")
        mpt_dve = sem("mpt_dve")
        mav_mm = sem("mav_mm")
        ot_ready = sem("ot_ready")
        ott_mm = sem("ott_mm")
        on_ready = sem("on_ready")
        ont_mm = sem("ont_mm")
        ont_ready = sem("ont_ready")
        proj_mm = sem("proj_mm")
        x_mha = sem("x_mha")
        stored = sem("stored")
        experts_in = [sem(f"experts_in{i}") for i in range(4)]
        x_v = x.rearrange("b (t p) d -> p (b t) d", p=P)
        out_v = out.rearrange("b (t p) d -> p (b t) d", p=P)
        wv_v = v_w.rearrange("n d p -> d n p")
        wo_v = o_w.rearrange("n p d -> p n d")
        SMALL = 9 * 16

        block = ctx.enter_context(nc.Block())

        @block.sync
        def _(sp):
            sp.dma_start(xs[:, 0:QT, :], x_v[:, 0:QT, :]).then_inc(x_first, 16)
            sp.dma_start(selraw[0:HE, :], sel_v_w).then_inc(small_in, 16)
            sp.dma_start(selraw[HE:2 * HE, :], sel_o_w).then_inc(small_in, 16)
            sp.dma_start(qraw[:], q_w.rearrange("(h p) d -> p h d", p=P)).then_inc(small_in, 16)
            sp.dma_start(kraw[:], k_w.rearrange("(h p) d -> p h d", p=P)).then_inc(small_in, 16)
            sp.dma_start(wraw[:], W_qkv.rearrange("(t p) d -> p t d", p=P)).then_inc(small_in, 16)
            sp.dma_start(woraw[:], W_out).then_inc(small_in, 16)
            sp.dma_start(braw[:], b_qkv.rearrange("(a n) -> a n", a=1)).then_inc(small_in, 16)
            sp.dma_start(bout[:], b_out.rearrange("(a n) -> a n", a=1)).then_inc(small_in, 16)
            sp.dma_start(rsraw[:], route_scale.rearrange("(a n) -> a n", a=1)).then_inc(small_in, 16)
            for n in range(2 * H):
                if n >= 4:
                    sp.wait_ge(raw_free, n - 3)
                src = (wv_v, wo_v)[n % 2][:, (n // 2) * E:(n // 2 + 1) * E, :]
                sp.dma_start(raw[:, n % 4], src).then_inc(experts_in[n % 4], 16)
            sp.dma_start(xs[:, QT:, :], x_v[:, QT:, :]).then_inc(x_rest, 16)
            with sp.Fori(0, B) as b:
                sp.wait_ge(x_ffn, b + (B + 2))
                sp.dma_start(out_v[:, bass.ts(b, QT), :], xs[:, bass.ts(b, QT), :]).then_inc(stored, 16)
            sp.wait_ge(stored, 16 * B)

        @block.tensor
        def _(pe):
            mm, tr = nc.tensor.matmul, nc.tensor.transpose

            def split3(o, hi, lo, rhi, rlo):
                mm(o, hi, rhi, start=True, stop=False)
                mm(o, hi, rlo, start=False, stop=False)
                return mm(o, lo, rhi, start=False, stop=True)

            def prep_transpose(n, free):
                pe.wait_ge(xn_ready, n + 1)
                free()
                for k in range(QT):
                    last = tr(qc[:, k * P:(k + 1) * P], xn[:, k, :], ident[:])
                last.then_inc(xt_mm, 1)

            def prep_logits(n):
                pe.wait_ge(xt_ready, n + 1)
                for k in range(QT):
                    last = mm(qc[:, k * P:(k + 1) * P], xT[:, k * P:(k + 1) * P], selT[:], start=True, stop=True)
                last.then_inc(lg_mm, 1)

            pe.wait_ge(small_in, SMALL)
            pe.wait_ge(ident_set, 1)
            tr(bank[0][:, 0:P], selraw[:], ident[:])
            tr(bank[0][:, P:2 * P], woraw[:], ident[:]).then_inc(tr_small, 1)
            for t in range(3):
                last = tr(bank[1][:, t * P:(t + 1) * P], wraw[:, t, :], ident[:])
            last.then_inc(tr_small, 1)
            for h in range(H):
                last = mm(bank[2 + h // 4][:, (h % 4) * P:(h % 4 + 1) * P], qraw[:, h, :], kraw[:, h, :],
                          start=True, stop=True)
            last.then_inc(mh_mm, 1)
            pe.wait_ge(ones_set, 1)
            pe.wait_ge(setup_rows, 1)
            for c in range(2 * NG + 2):
                mm(bank[4][:, c:c + 1], brow[0:1, c, :], ones[0:1, 0:1], start=True, stop=True)
            mm(bank[5][:, 0:NH * DH], ones[0:1, :], bvrow[0:1, :], start=True, stop=True)
            mm(bank[5][:, P:P + 1], ones[0:1, :], rsraw[0:1, :], start=True, stop=True).then_inc(rows_mm, 1)
            prep_transpose(0, lambda: None)
            pe.wait_ge(sel_ready, 1)
            prep_logits(0)

            def ffn_stage(f, b):
                n = 4 * f + b
                t = 8 * f + b
                q, s_, u = 8 * n, UNITS * n, UNITS * n

                def query(h):
                    if h >= 2:
                        pe.wait_ge(c_lo, q + h - 1)
                    if h == 4:
                        pe.wait_ge(lg_exp, t + 2)
                    split3(qc[:], mh[:, 0, h, :], mh[:, 1, h, :], xhl[:, 0, :], xhl[:, 1, :]).then_inc(q_mm, 1)

                def score(h, k):
                    i = QT * h + k
                    if k == 0:
                        pe.wait_ge(q_lo, q + h + 1)
                    if i >= 2:
                        pe.wait_ge(s_exp, s_ + i - 1)
                    c = slice(k * P, (k + 1) * P)
                    split3(sbk[i % 2][:], qhl[:, 0, c], qhl[:, 1, c], xhl[:, 0, :], xhl[:, 1, :]).then_inc(s_mm, 1)

                def values(h, k, half):
                    i = QT * h + k
                    c = slice(k * P, (k + 1) * P)
                    done, free = ((v0_mm, v_act), (v1_mm, v_dve))[half]
                    if i >= 1:
                        pe.wait_ge(free, u + i)
                    e = slice(h * E + half * G, h * E + (half + 1) * G)
                    split3(gb[half][:], xhl[:, 0, c], xhl[:, 1, c], wv[:, 0, e, :], wv[:, 1, e, :]).then_inc(done, 1)

                def transposes(h, k):
                    i = QT * h + k
                    pe.wait_ge(s_exp, s_ + i + 1)
                    if i >= 1:
                        pe.wait_ge((pt_dve, pt_act)[(i - 1) % 2], 16 * n + (i - 1) // 2 + 1)
                    for c in range(QT):
                        last = tr(tb[:, c * P:(c + 1) * P], pp[:, i % 2, c * P:(c + 1) * P], ident[:])
                    last.then_inc(t_mm, 1)

                def context(h):
                    pe.wait_ge(pt_act, 16 * n + 2 * h + 2)
                    pe.wait_ge(pt_dve, 16 * n + 2 * h + 2)
                    pe.wait_ge(v_fold, u + QT * (h + 1))
                    if h < H - 1:
                        pe.wait_ge(q_lo, q + h + 2)
                    for c in range(QT):
                        last = mm(qc[:], vv[:, h % 2, c, :], pt[:, c, :], start=(c == 0), stop=(c == QT - 1))
                    last.then_inc(av_mm, 1)

                def outputs(h, k, half):
                    i = QT * h + k
                    c = slice(k * P, (k + 1) * P)
                    done, free = ((o0_mm, o_act), (o1_mm, o_dve))[half]
                    if k == 0 and half == 0:
                        pe.wait_ge(c_lo, q + h + 1)
                    if i == 0 and half == 0:
                        pe.wait_ge(x_ffn, n + 1)
                    if i >= 1:
                        pe.wait_ge(free, u + i)
                    e = slice(h * E + half * G, h * E + (half + 1) * G)
                    split3(gb[2 + half][:], chl[:, 0, c], chl[:, 1, c], wo[:, 0, e, :], wo[:, 1, e, :]).then_inc(done, 1)

                pe.wait_ge(prep_done, t + 1)
                if f == 1:
                    pe.wait_ge(x_mha, B + 1)
                query(0)
                for k in range(QT):
                    values(0, k, 0)
                    values(0, k, 1)
                for h in range(H):
                    more, past = h < H - 1, h >= 1
                    for k in range(QT):
                        if more:
                            values(h + 1, k, 0)
                        if past and k > 0:
                            outputs(h - 1, k, 0)
                        score(h, k)
                        if more and k == QT - 1:
                            query(h + 1)
                        if k >= 1:
                            transposes(h, k - 1)
                        if more:
                            values(h + 1, k, 1)
                        if past and k == 0:
                            outputs(h - 1, k, 0)
                        if k == QT - 1:
                            transposes(h, k)
                        if past:
                            outputs(h - 1, k, 1)
                        if (h, k) == (3, 0):
                            prep_transpose(t + 1, lambda: pe.wait_ge(c_lo, q + 3))
                        if (h, k) == (3, 1):
                            prep_logits(t + 1)
                    context(h)
                for k in range(QT):
                    outputs(H - 1, k, 0)
                    outputs(H - 1, k, 1)

            def mha_stage(b):
                t = B + b
                m = MU * b

                def stack(g):
                    for c, w in enumerate((wqs, wks)):
                        n = 2 * g + c
                        if n >= 1:
                            pe.wait_ge(qkf_ready, 2 * NG * b + n)
                        mm(qc[:], w[:, g, :], xT[:], start=True, stop=True).then_inc(qk_mm, 1)

                def score(i):
                    g, k, j = i // (QT * GH), i // GH % QT, i % GH
                    if i % (QT * GH) == 0:
                        pe.wait_ge(qk_ready, 2 * NG * b + 2 * g + 2)
                    if i >= GH:
                        pe.wait_ge(m_exp, m + i - GH + 1)
                    r = slice(R * j, R * j + R)
                    mm(bank[j][:], qk[r, g % 2, 0, k * P:(k + 1) * P], qk[r, g % 2, 1, :],
                       start=True, stop=True).then_inc(ms_mm, 1)

                def transposes(i):
                    pe.wait_ge(m_exp, m + i + 1)
                    if i >= 2:
                        pe.wait_ge((mpt_act, mpt_dve)[i % 2], MU // 2 * b + i // 2)
                    for c in range(QT):
                        last = tr(sbk[i % 2][:, c * P:(c + 1) * P], pm[:, i % GH, c * P:(c + 1) * P], ident[:])
                    last.then_inc(mt_mm, 1)

                def context(g, k):
                    a = QT * g + k
                    pe.wait_ge(mpt_act, MU // 2 * b + GH // 2 * (a + 1))
                    pe.wait_ge(mpt_dve, MU // 2 * b + GH // 2 * (a + 1))
                    if k == 0 and g == 0:
                        pe.wait_ge(vext_ready, b + 1)
                    if k == 0 and g >= 1:
                        pe.wait_ge(ot_ready, NG * b + g)
                    for c in range(QT):
                        for j in range(GH):
                            last = mm(tb[R * j:R * j + R, k * P:(k + 1) * P], vext[:, c, GH * g + j, :],
                                      ptm[:, j, c, :], start=(c == 0), stop=(c == QT - 1), skip_group_check=True)
                    last.then_inc(mav_mm, 1)

                def out_transposes(g):
                    pe.wait_ge(ot_ready, NG * b + g + 1)
                    if g < NG - 1:
                        pe.wait_ge(qkf_ready, 2 * NG * b + 2 * min(g + 2, NG))
                    for k in range(QT):
                        last = tr(qc[:, k * P:(k + 1) * P], oT[:, k * P:(k + 1) * P], ident[:])
                    last.then_inc(ott_mm, 1)

                pe.wait_ge(xt_ready, t + 1)
                pe.wait_ge(lg_exp, t + 1)
                pe.wait_ge(prep_done, t + 1)
                pe.wait_ge(x_ffn, B + 1)
                pe.wait_ge(x_mha, b + 1)
                for k in range(QT):
                    last = mm(qc[:, k * P:(k + 1) * P], xT[:, k * P:(k + 1) * P], wvT[:], start=True, stop=True)
                last.then_inc(mv_mm, 1)
                pe.wait_ge(vext_ready, b + 1)
                stack(0)
                LEAD = 3
                for i in range(LEAD):
                    score(i)
                for i in range(MU):
                    g, u = i // (QT * GH), i % (QT * GH)
                    if i + LEAD < MU:
                        score(i + LEAD)
                    transposes(i)
                    if i % GH == 0 and i >= GH:
                        a = i // GH - 1
                        context(a // QT, a % QT)
                    if g >= 1 and u == 3:
                        out_transposes(g - 1)
                    if g < NG - 1 and u == 6:
                        if g >= 1:
                            pe.wait_ge(on_ready, NG * b + g)
                        stack(g + 1)
                    if g == NG - 1 and u == 6:
                        prep_transpose(t + 1, lambda: pe.wait_ge(on_ready, NG * b + NG - 1))
                    if g == NG - 1 and u == 9:
                        prep_logits(t + 1)
                context(NG - 1, QT - 1)
                pe.wait_ge(lg_exp, t + 2)
                out_transposes(NG - 1)
                pe.wait_ge(on_ready, NG * b + NG)
                for k in range(QT):
                    last = tr(sbk[0][:, k * P:(k + 1) * P], oN[:, k, :, :].rearrange("p h d -> p (h d)"), ident[:])
                last.then_inc(ont_mm, 1)
                pe.wait_ge(ont_ready, b + 1)
                for k in range(QT):
                    o = sbk[1][:, k * P:(k + 1) * P]
                    mm(o, oT[:, k * P:(k + 1) * P], woT[:], start=True, stop=False)
                    last = mm(o, ones[0:1, :], bout[0:1, :], start=False, stop=True)
                last.then_inc(proj_mm, 1)

            with pe.Fori(0, B) as b:
                ffn_stage(0, b)
            with pe.Fori(0, B) as b:
                mha_stage(b)
            with pe.Fori(0, B) as b:
                ffn_stage(1, b)

        @block.scalar
        def _(act):
            activation = nc.scalar.activation

            def prep(n):
                act.wait_ge(xt_mm, n + 1)
                activation(xT[:], qc[:], ACT.Copy).then_inc(xt_ready, 1)

            def prep_exp(n):
                act.wait_ge(lg_mm, n + 1)
                activation(xn[:].rearrange("p t d -> p (t d)"), qc[:], ACT.Exp, scale=-1.0).then_inc(lg_exp, 1)

            act.wait_ge(mh_mm, 1)
            for h in range(2):
                last = activation(mf[:, 4 * h:4 * h + 4, :].rearrange("p h d -> p (h d)"), bank[2 + h][:], ACT.Copy,
                                  scale=-FFN_SCALE)
            last.then_inc(mh_scaled, 1)
            prep(0)
            prep_exp(0)
            for n in range(2 * H):
                act.wait_ge(experts_in[n % 4], 16 * (n // 4 + 1))
                w = (wv, wo)[n % 2]
                h = n // 2
                activation(w[:, 0, h * E:(h + 1) * E, :], raw[:, n % 4], ACT.Copy).then_inc(act_setup, 1)

            def ffn_stage(f, b):
                n = 4 * f + b
                t = 8 * f + b
                q, u = 8 * n, UNITS * n

                def query(h):
                    act.wait_ge(q_mm, q + h + 1)
                    activation(qhl[:, 0, :], qc[:], ACT.Copy).then_inc(q_hi, 1)

                def context(h):
                    act.wait_ge(av_mm, q + h + 1)
                    activation(chl[:, 0, :], qc[:], ACT.Copy).then_inc(c_hi, 1)

                def values(h, k):
                    i = QT * h + k
                    act.wait_ge(v0_mm, u + i + 1)
                    if i >= 2:
                        act.wait_ge(v_fold, u + i - 1)
                    for e in range(G):
                        last = activation(vt[:, i % 2, e * P:(e + 1) * P], gb[0][:, e * P:(e + 1) * P], ACT.Copy,
                                          scale=gate[:, k, h * E + e:h * E + e + 1])
                    last.then_inc(v_act, 1)

                def softmax(h, k):
                    i = QT * h + k
                    act.wait_ge(s_min, u + i + 1)
                    if i >= 2:
                        act.wait_ge(t_mm, u + i - 1)
                    activation(pp[:, i % 2, :], sbk[i % 2][:], ACT.Exp, bias=nmin[:, h % 2, k:k + 1], scale=-1.0,
                               accum_out=den[:, h % 2, k:k + 1]).then_inc(s_exp, 1)

                def copy_pt(h, k):
                    i = QT * h + k
                    act.wait_ge(t_mm, u + i + 1)
                    if k == 1 and h >= 1:
                        act.wait_ge(av_mm, q + h)
                    activation(pt[:, :, k * P:(k + 1) * P], tb[:].rearrange("p (c q) -> p c q", c=QT),
                               ACT.Copy).then_inc(pt_act, 1)

                def outputs(h, k):
                    i = QT * h + k
                    act.wait_ge(o0_mm, u + i + 1)
                    if k == 0:
                        act.wait_ge(gn_ready, q + h + 1)
                    if h >= 1 and i - QT >= 2:
                        act.wait_ge(o_acc, (UNITS - QT) * n + i - QT - 1)
                    o = acc[:, k, :] if h == 0 else ot[:, i % 2, :]
                    for e in range(G):
                        last = activation(o[:, e * D:(e + 1) * D], gb[2][:, e * D:(e + 1) * D], ACT.Copy,
                                          scale=gn[:, h % 2, k, e:e + 1])
                    last.then_inc(o_act, 1)

                act.wait_ge(prep_done, t + 1)
                if f == 1:
                    act.wait_ge(x_mha, B + 1)
                query(0)
                for k in range(QT):
                    values(0, k)
                for h in range(H):
                    more, past = h < H - 1, h >= 1
                    for k in range(QT):
                        if more:
                            values(h + 1, k)
                        if past and k > 0:
                            outputs(h - 1, k)
                        softmax(h, k)
                        if more and k == QT - 1:
                            query(h + 1)
                        if past and k == 0:
                            outputs(h - 1, k)
                        if k == 2:
                            copy_pt(h, 1)
                        if (h, k) == (3, 0):
                            prep(t + 1)
                        if (h, k) == (3, 2):
                            prep_exp(t + 1)
                    copy_pt(h, QT - 1)
                    context(h)
                for k in range(QT):
                    outputs(H - 1, k)

            def mha_stage(b):
                t = B + b
                m = MU * b

                def stack(g):
                    for c in range(2):
                        n = 2 * g + c
                        act.wait_ge(qk_mm, 2 * NG * b + n + 1)
                        if n >= 2:
                            act.wait_ge(qk_ready, 2 * NG * b + n - 1)
                        activation(qkf[:, c, :], qc[:], ACT.Identity,
                                   bias=bst[:, c * NG + g:c * NG + g + 1]).then_inc(qkf_ready, 1)

                def softmax(i):
                    act.wait_ge(m_max, m + i + 1)
                    if i >= GH:
                        act.wait_ge(mt_mm, m + i - GH + 1)
                    activation(pm[:, i % GH, :], bank[i % GH][:], ACT.Exp,
                               bias=mmax[:, i % GH:i % GH + 1], scale=-1.0).then_inc(m_exp, 1)

                def copy_pt(i):
                    act.wait_ge(mt_mm, m + i + 1)
                    if i >= GH:
                        act.wait_ge(mav_mm, QT * NG * b + i // GH)
                    activation(ptm[:, i % GH, :, :].rearrange("p c q -> p (c q)"), sbk[i % 2][:],
                               ACT.Copy).then_inc(mpt_act, 1)

                def copy_out(g):
                    act.wait_ge(mav_mm, QT * NG * b + QT * (g + 1))
                    if g >= 1:
                        act.wait_ge(ott_mm, NG * b + g)
                    activation(oT[:], tb[:], ACT.Copy).then_inc(ot_ready, 1)

                act.wait_ge(x_ffn, B + 1)
                act.wait_ge(x_mha, b + 1)
                stack(0)
                for i in range(MU):
                    g, u = i // (QT * GH), i % (QT * GH)
                    softmax(i)
                    if i % 2 == 1:
                        copy_pt(i - 1)
                    if g >= 1 and u == 1:
                        copy_out(g - 1)
                    if g < NG - 1 and u == 7:
                        stack(g + 1)
                    if g == NG - 1 and u == 7:
                        prep(t + 1)
                    if g == NG - 1 and u == 10:
                        prep_exp(t + 1)
                copy_out(NG - 1)
                act.wait_ge(ont_mm, b + 1)
                activation(oT[:], sbk[0][:], ACT.Copy).then_inc(ont_ready, 1)

            with act.Fori(0, B) as b:
                ffn_stage(0, b)
            with act.Fori(0, B) as b:
                mha_stage(b)
            with act.Fori(0, B) as b:
                ffn_stage(1, b)

        @block.vector
        def _(dve):
            v = nc.vector
            own = Chain(dve, dve_own)
            PREP = 12 + 3 * (E - 1)
            FFN_OWN = PREP + H
            MHA_OWN = PREP + 3 * NG
            M = QT * 2 * H
            pr = xn[:].rearrange("p t (g e) -> p (t g) e", e=E)

            def statistics(nb):
                for k in range(QT):
                    last = v.bn_stats(st[:, k, :], xs[:, nb * QT + k, :])
                own.link(last)
                v.memset(tick[:], 0.0)
                for k in range(QT):
                    last = v.bn_aggr(mv[:, k, :], st[:, k, :])
                last.then_inc(mv_ready, 1)

            def normalise(n, nb):
                dve.wait_ge(rstd_ready, n + 1)
                for k in range(QT):
                    last = v.tensor_scalar(xn[:, k, :], xs[:, nb * QT + k, :], mv[:, k, 0:1], rstd[:, k:k + 1],
                                           ALU.subtract, ALU.mult)
                last.then_inc(xn_ready, 1)

            def sigmoids(n):
                dve.wait_ge(lg_exp, n + 1)
                own.link(v.memset(cnt[:], 0.0))
                own.link(v.tensor_scalar_add(pr, pr, 1.0))
                own.link(v.reciprocal(pr, pr))

            def ranks(*distances):
                for k in distances:
                    own.link(v.tensor_tensor(cmp_[:, :, 0:E - k], pr[:, :, 0:E - k], pr[:, :, k:E], ALU.is_ge))
                    own.link(v.tensor_tensor(cnt[:, :, k:E], cnt[:, :, k:E], cmp_[:, :, 0:E - k], ALU.add))
                    own.link(v.tensor_tensor(cnt[:, :, 0:E - k], cnt[:, :, 0:E - k], cmp_[:, :, 0:E - k], ALU.subtract))

            def weights():
                own.link(v.tensor_tensor(cmp_[:], cnt[:], thr[:].unsqueeze(1).to_broadcast([P, M, E]), ALU.is_lt))
                own.link(v.tensor_tensor(pr, pr, cmp_[:], ALU.mult))
                own.link(v.tensor_reduce(gsum[:], pr, AX.X, ALU.add))
                own.link(v.tensor_scalar_max(gsum[:], gsum[:], 1e-9))
                own.link(v.reciprocal(gsum[:], gsum[:]))
                own.link(v.tensor_tensor(gsum[:].rearrange("p (t g) -> p t g", t=QT),
                                         gsum[:].rearrange("p (t g) -> p t g", t=QT),
                                         rsb[:].unsqueeze(1).to_broadcast([P, QT, 2 * H]), ALU.mult))
                own.link(v.tensor_tensor(pr, pr, gsum[:].unsqueeze(2).to_broadcast([P, M, E]), ALU.mult))

            def gates(n):
                sigmoids(n)
                ranks(*range(1, E))
                weights()

            def commit(free):
                free()
                v.tensor_copy(gate[:].rearrange("p t d -> p (t d)"), xn[:].rearrange("p t d -> p (t d)"))
                own.link(v.tensor_copy(xhl[:, 0, :], xT[:]))
                v.tensor_tensor(xhl[:, 1, :], xT[:], xhl[:, 0, :].bitcast(F32), ALU.subtract).then_inc(prep_done, 1)

            v.memset(ones[:], 1.0)
            v.memset(ph[:], -0.5)
            v.memset(eps[:], LN_EPS)
            v.memset(wqs[:], 0.0)
            v.memset(wks[:], 0.0)
            for e in range(E):
                v.memset(thr[:, e:e + 1], float(e - (E - 3)))
            own.link(v.memset(brow[:], 0.0))
            v.tensor_copy(ones[:], ones[:]).then_inc(ones_set, 1)
            v.memset(gsum[:], 0.0).then_inc(x_mha, 1)
            dve.wait_ge(x_first, 16)
            statistics(0)
            normalise(0, 0)
            dve.wait_ge(small_in, SMALL)
            heads = braw[:].rearrange("p (h c) -> p h c", h=NH)
            for r in range(3):
                c = slice(DH * r, DH * r + DH)
                v.tensor_scalar_mul(brow[0:1, 0:NG, :].rearrange("p g (j r) -> p (g j) r", j=GH)[:, :, c],
                                    heads[:, :, 0:DH], -MHA_SCALE)
                v.tensor_copy(brow[0:1, NG:2 * NG, :].rearrange("p g (j r) -> p (g j) r", j=GH)[:, :, c],
                              heads[:, :, DH:2 * DH])
            v.memset(brow[0:1, 2 * NG, :].rearrange("p (j r) -> p j r", j=GH)[:, :, 2 * DH:3 * DH], -1.0)
            v.memset(brow[0:1, 2 * NG + 1, :].rearrange("p (j r) -> p j r", j=GH)[:, :, DH:2 * DH], -1.0)
            v.tensor_copy(bvrow[:].rearrange("p (h c) -> p h c", h=NH), heads[:, :, 2 * DH:3 * DH]).then_inc(setup_rows, 1)
            dve.wait_ge(tr_small, 2)
            v.tensor_copy(selT[:], bank[0][:, 0:P]).then_inc(sel_ready, 1)
            v.tensor_copy(woT[:], bank[0][:, P:2 * P])
            wh = bank[1][:, 0:3 * P].rearrange("p (h c) -> p h c", h=NH)
            for r in range(3):
                c = slice(DH * r, DH * r + DH)
                v.tensor_scalar_mul(wqs[:].rearrange("p g (j r) -> p (g j) r", j=GH)[:, :, c], wh[:, :, 0:DH], -MHA_SCALE)
                v.tensor_copy(wks[:].rearrange("p g (j r) -> p (g j) r", j=GH)[:, :, c], wh[:, :, DH:2 * DH])
            v.tensor_copy(wvT[:].rearrange("p (h c) -> p h c", h=NH), wh[:, :, 2 * DH:3 * DH])
            dve.wait_ge(rows_mm, 1)
            v.tensor_copy(bst[:], bank[4][:, 0:2 * NG + 2])
            v.tensor_copy(bvb[:], bank[5][:, 0:NH * DH])
            v.tensor_copy(rsb[:, 0:H], bank[5][:, P:P + 1].to_broadcast([P, H]))
            own.link(v.tensor_scalar_mul(rsb[:, H:2 * H], bank[5][:, P:P + 1].to_broadcast([P, H]), 0.5))
            dve.wait_ge(mh_scaled, 1)
            own.link(v.tensor_copy(mh[:, 0, :, :], mf[:]))
            v.tensor_tensor(mh[:, 1, :, :], mf[:], mh[:, 0, :, :].bitcast(F32), ALU.subtract)
            gates(0)
            for n in range(2 * H):
                w = (wv, wo)[n % 2]
                h = n // 2
                dve.wait_ge(act_setup, n + 1)
                v.tensor_tensor(w[:, 1, h * E:(h + 1) * E, :], raw[:, n % 4],
                                w[:, 0, h * E:(h + 1) * E, :].bitcast(F32), ALU.subtract).then_inc(raw_free, 1)
            commit(lambda: None)
            dve.wait_ge(x_rest, 16)

            def ffn_stage(f, b):
                n = 4 * f + b
                t = 8 * f + b
                q, u = 8 * n, UNITS * n
                nb = (b + 1) % B

                def query(h):
                    dve.wait_ge(q_hi, q + h + 1)
                    v.tensor_tensor(qhl[:, 1, :], qc[:], qhl[:, 0, :].bitcast(F32), ALU.subtract).then_inc(q_lo, 1)

                def context(h):
                    dve.wait_ge(c_hi, q + h + 1)
                    v.tensor_tensor(chl[:, 1, :], qc[:], chl[:, 0, :].bitcast(F32), ALU.subtract).then_inc(c_lo, 1)

                def row_max(h, k):
                    i = QT * h + k
                    dve.wait_ge(s_mm, u + i + 1)
                    v.tensor_reduce(nmin[:, h % 2, k:k + 1], sbk[i % 2][:], AX.X, ALU.min).then_inc(s_min, 1)

                def values(h, k):
                    i = QT * h + k
                    dve.wait_ge(v1_mm, u + i + 1)
                    dve.wait_ge(v_act, u + i + 1)
                    for e in range(G):
                        o = vt[:, i % 2, e * P:(e + 1) * P]
                        last = v.scalar_tensor_tensor(o, gb[1][:, e * P:(e + 1) * P],
                                                      gate[:, k, h * E + G + e:h * E + G + e + 1], o, ALU.mult, ALU.add)
                    last.then_inc(v_dve, 1)

                def outputs(h, k):
                    i = QT * h + k
                    dve.wait_ge(o1_mm, u + i + 1)
                    dve.wait_ge(o_act, u + i + 1)
                    if k == 0:
                        dve.wait_ge(gn_ready, q + h + 1)
                    row = acc[:, k, :] if h == 0 else ot[:, i % 2, :]
                    for e in range(G):
                        o = row[:, e * D:(e + 1) * D]
                        last = v.scalar_tensor_tensor(o, gb[3][:, e * D:(e + 1) * D],
                                                      gn[:, h % 2, k, G + e:G + e + 1], o, ALU.mult, ALU.add)
                    last.then_inc(o_dve, 1)

                def copy_pt(h, k):
                    i = QT * h + k
                    dve.wait_ge(t_mm, u + i + 1)
                    if k == 0 and h >= 1:
                        dve.wait_ge(av_mm, q + h)
                    v.tensor_copy(pt[:, :, k * P:(k + 1) * P], tb[:].rearrange("p (c q) -> p c q", c=QT))\
                        .then_inc(pt_dve, 1)

                def output_gates(h):
                    dve.wait_ge(s_exp, u + QT * (h + 1))
                    own.link(v.reciprocal(rden[:, h % 2, :], den[:, h % 2, :]))
                    v.tensor_tensor(gn[:, h % 2, :, :], gate[:, :, HE + h * E:HE + (h + 1) * E],
                                             rden[:, h % 2, :].unsqueeze(2).to_broadcast([P, QT, E]), ALU.mult)\
                        .then_inc(gn_ready, 1)

                if f == 1:
                    dve.wait_ge(x_mha, B + 1)
                query(0)
                for k in range(QT):
                    values(0, k)
                for h in range(H):
                    more, past = h < H - 1, h >= 1
                    for k in range(QT):
                        row_max(h, k)
                        if k % 2 == 1:
                            copy_pt(h, k - 1)
                        if more and k == QT - 1:
                            query(h + 1)
                        if more:
                            values(h + 1, k)
                        if past:
                            outputs(h - 1, k)
                    if h == 1:
                        dve.wait_ge(x_ffn, n + 1)
                        statistics(nb)
                    if h == 2:
                        normalise(t + 1, nb)
                    output_gates(h)
                    if h == 3:
                        sigmoids(t + 1)
                    if h in (4, 5, 6):
                        ranks(*((1, 2), (3, 4), (5, 6, 7))[h - 4])
                    if h == 7:
                        weights()
                    context(h)
                commit(lambda: dve.wait_ge(gn_ready, q + H))
                for k in range(QT):
                    outputs(H - 1, k)

            def mha_stage(b):
                t = B + b
                m = MU * b
                nb = (b + 1) % B

                def stack(g):
                    for c in range(2):
                        dve.wait_ge(qkf_ready, 2 * NG * b + 2 * g + c + 1)
                        if g >= 2:
                            dve.wait_ge(ms_mm, m + QT * GH * (g - 1))
                        o = qk[:, g % 2, c, :]
                        own.link(v.tensor_copy(o, qkf[:, c, :]))
                        v.scalar_tensor_tensor(o, o.bitcast(F32), bst[:, 2 * NG + c:2 * NG + c + 1], qkf[:, c, :],
                                               ALU.mult, ALU.add).then_inc(qk_ready, 1)

                def row_max(i):
                    dve.wait_ge(ms_mm, m + i + 1)
                    v.tensor_reduce(mmax[:, i % GH:i % GH + 1], bank[i % GH][:], AX.X, ALU.min).then_inc(m_max, 1)

                def copy_pt(i):
                    dve.wait_ge(mt_mm, m + i + 1)
                    if i >= GH:
                        dve.wait_ge(mav_mm, QT * NG * b + i // GH)
                    v.tensor_copy(ptm[:, i % GH, :, :].rearrange("p c q -> p (c q)"), sbk[i % 2][:])\
                        .then_inc(mpt_dve, 1)

                def over_sums(g):
                    dve.wait_ge(ott_mm, NG * b + g + 1)
                    o = qc[:].rearrange("p (k j r) -> p k j r", k=QT, j=GH)
                    own.link(v.reciprocal(mrd[:], o[:, :, :, DH]))
                    v.tensor_tensor(oN[:, :, GH * g:GH * g + GH, :], o[:, :, :, 0:DH],
                                    mrd[:].unsqueeze(3).to_broadcast([P, QT, GH, DH]), ALU.mult).then_inc(on_ready, 1)

                dve.wait_ge(x_ffn, B + 1)
                v.memset(vext[:, :, :, DH:DH + 1], 1.0)
                v.memset(vext[:, :, :, DH + 1:R], 0.0)
                dve.wait_ge(mv_mm, b + 1)
                v.tensor_tensor(vext[:, :, :, 0:DH], qc[:].rearrange("p (k h c) -> p k h c", k=QT, h=NH),
                                bvb[:].rearrange("p (h c) -> p h c", h=NH).unsqueeze(1).to_broadcast([P, QT, NH, DH]),
                                ALU.add).then_inc(vext_ready, 1)
                stack(0)
                for i in range(MU):
                    g, u = i // (QT * GH), i % (QT * GH)
                    row_max(i)
                    if i % 2 == 0 and i >= 2:
                        copy_pt(i - 1)
                    if g >= 1 and u == 4:
                        over_sums(g - 1)
                    if g < NG - 1 and u == 8:
                        stack(g + 1)
                    if g == 2 and u == 6:
                        statistics(nb)
                    if g == 2 and u == 12:
                        normalise(t + 1, nb)
                    if g == NG - 1 and u == 11:
                        gates(t + 1)
                copy_pt(MU - 1)
                over_sums(NG - 1)
                commit(lambda: None)
                dve.wait_ge(proj_mm, b + 1)
                xb = xs[:, bass.ts(b, QT), :]
                v.tensor_tensor(xb, xb, sbk[1][:].rearrange("p (k d) -> p k d", k=QT), ALU.add).then_inc(x_mha, 1)

            with dve.Fori(0, B) as b:
                own.enter(b, FFN_OWN)
                ffn_stage(0, b)
            own.leave(B)
            with dve.Fori(0, B) as b:
                own.enter(b, MHA_OWN)
                mha_stage(b)
            own.leave(B)
            with dve.Fori(0, B) as b:
                own.enter(b, FFN_OWN)
                ffn_stage(1, b)
            own.leave(B)

        @block.gpsimd
        def _(pool):
            g_ = nc.gpsimd
            own = Chain(pool, pool_own)
            PREP = 1

            def rstd_(n):
                pool.wait_ge(mv_ready, n + 1)
                own.link(g_.tensor_tensor(ve[:], mv[:, :, 1], eps[:], ALU.add))
                g_.tensor_tensor(rstd[:], ve[:], ph[:], ALU.pow).then_inc(rstd_ready, 1)

            own.link(g_.memset(ident[:], 0.0))
            g_.affine_select(out=ident[:], in_=ident[:], compare_op=ALU.not_equal, fill=1.0, base=0,
                             pattern=[[-1, P]], channel_multiplier=1).then_inc(ident_set, 1)
            g_.memset(ptick[:], 0.0).then_inc(x_ffn, 1)
            pool.wait_ge(ones_set, 1)
            rstd_(0)

            def ffn_stage(f, b):
                n = 4 * f + b
                t = 8 * f + b
                u = UNITS * n

                def fold_values(h, k):
                    i = QT * h + k
                    pool.wait_ge(v_dve, u + i + 1)
                    a = vt[:, i % 2, :]
                    own.link(g_.tensor_tensor(a[:, 0:2 * P], a[:, 0:2 * P], a[:, 2 * P:4 * P], ALU.add))
                    if k == 0 and h >= 2:
                        pool.wait_ge(av_mm, 8 * n + h - 1)
                    g_.tensor_tensor(vv[:, h % 2, k, :], a[:, 0:P], a[:, P:2 * P], ALU.add).then_inc(v_fold, 1)

                def add_outputs(h, k):
                    i = QT * h + k
                    pool.wait_ge(o_dve, u + i + 1)
                    g_.tensor_tensor(acc[:, k, :], acc[:, k, :], ot[:, i % 2, :], ALU.add).then_inc(o_acc, 1)

                for k in range(QT):
                    fold_values(0, k)
                for h in range(H):
                    for k in range(QT):
                        if h < H - 1:
                            fold_values(h + 1, k)
                        if h >= 2:
                            add_outputs(h - 1, k)
                    if h == 1:
                        rstd_(t + 1)
                for k in range(QT):
                    add_outputs(H - 1, k)
                pool.wait_ge(o_acc, (UNITS - QT) * (n + 1))
                own.link(g_.tensor_tensor(acc[:, :, 0:2 * D], acc[:, :, 0:2 * D], acc[:, :, 2 * D:4 * D], ALU.add))
                own.link(g_.tensor_tensor(acc[:, :, 0:D], acc[:, :, 0:D], acc[:, :, D:2 * D], ALU.add))
                xb = xs[:, bass.ts(b, QT), :]
                g_.tensor_tensor(xb, xb, acc[:, :, 0:D], ALU.add).then_inc(x_ffn, 1)

            FFN_OWN = UNITS + PREP + 2
            with pool.Fori(0, B) as b:
                own.enter(b, FFN_OWN)
                ffn_stage(0, b)
            own.leave(B)
            with pool.Fori(0, B) as b:
                own.enter(b, PREP)
                rstd_(B + b + 1)
            own.leave(B)
            with pool.Fori(0, B) as b:
                own.enter(b, FFN_OWN)
                ffn_stage(1, b)
            own.leave(B)


_INS = ["L0_attn_x", "L0_attn_W_qkv", "L0_attn_b_qkv", "L0_attn_W_out", "L0_attn_b_out", "L0_ffn_q_w", "L0_ffn_k_w",
        "L0_ffn_v_w", "L0_ffn_o_w", "L0_ffn_sel_v_w", "L0_ffn_sel_o_w", "L0_ffn_route_scale"]


def kernel(**inputs):
    import concourse.bacc as bacc
    from concourse.bass_utils import run_bass_kernel_spmd

    nc = bacc.Bacc("TRN2", target_bir_lowering=False, num_devices=1)
    arrays, args = {}, []
    for name in _INS:
        a = np.ascontiguousarray(inputs[name])
        arrays[f"in_{name}"] = a
        args.append(nc.dram_tensor(f"in_{name}", a.shape, mybir.dt.from_np(a.dtype), kind="ExternalInput").ap())
    out = nc.dram_tensor("out_x", (B, S, D), F32, kind="ExternalOutput").ap()
    macaron_kernel(nc, *args, out)
    r = run_bass_kernel_spmd(nc, [arrays], core_ids=[0])
    return r.results[0]["out_x"]
```

```python
from contextlib import ExitStack

import numpy as np
import concourse.bass as bass
from concourse import mybir

F32 = mybir.dt.float32
F32R = mybir.dt.float32r
BF16 = mybir.dt.bfloat16
ALU = mybir.AluOpType
ACT = mybir.ActivationFunctionType
AX = mybir.AxisListType

B, S, D = 4, 512, 128
P = 128
QT = S // P
H, E = 8, 8
HE = H * E
G = 4
NH, DH = 16, 8
NG, GH = 4, 4
R = 32
LN_EPS = 1e-5
FFN_SCALE = 1.0 / float(np.sqrt(P))
MHA_SCALE = 1.0 / float(np.sqrt(DH))
UNITS = H * QT
GU = QT * GH
MU = NG * GU
LAG = 26
V_STEP, PROJ_STEP = 29, 39
TAIL = 41

FLOW = []
for _s in range(MU):
    FLOW += [("values", 0)] * (_s == V_STEP) + [("output", 0)] * (_s == PROJ_STEP) + [("score", _s)]
PLACE = {what: at for at, what in enumerate(FLOW)}
assert len(FLOW) % 3 == 0


class Chain:

    def __init__(self, eng, sem):
        self.eng, self.sem, self.done, self.base = eng, sem, 0, 0

    def then(self, ins):
        ins.then_inc(self.sem, 1)
        self.done += 1
        return ins

    def settle(self):
        self.eng.wait_ge(self.sem, self.base + self.done)

    def link(self, ins):
        self.then(ins)
        self.settle()

    def enter(self, i, per):
        self.before, self.per = self.done + 0, per
        self.base, self.done = i * per + self.before, 0

    def leave(self, trips):
        assert self.done == self.per, (self.done, self.per)
        self.base, self.done = 0, self.before + trips * self.per


def macaron_kernel(nc, x, W_qkv, b_qkv, W_out, b_out, q_w, k_w, v_w, o_w, sel_v_w, sel_o_w, route_scale, out):
    ctx = ExitStack()
    with ctx:
        def sb(name, shape, dt=F32, at=ctx):
            return at.enter_context(nc.sbuf_tensor(name, shape, dt))

        def sem(name):
            return ctx.enter_context(nc.semaphore(name))

        xs = sb("xs", [P, B * QT, D])
        wv = sb("wv", [P, 2, HE, P], F32R)
        wo = sb("wo", [P, 2, HE, D], F32R)
        mh = sb("mh", [P, 2, H, D], F32R)
        ident = sb("ident", [P, P])
        selT = sb("selT", [D, 2 * HE])
        wqs = sb("wqs", [D, NG, P])
        wks = sb("wks", [D, NG, P])
        wvT = sb("wvT", [D, NH * DH])
        woT = sb("woT", [NH * DH, D])
        bvb = sb("bvb", [P, NH * DH])
        bout = sb("bout", [1, D])
        bst = sb("bst", [P, 2 * NG + 2])
        ones = sb("ones", [1, P])
        thr = sb("thr", [P, E])
        rsb = sb("rsb", [P, 2 * H])
        ph = sb("ph", [P, QT])
        eps = sb("eps", [P, QT])
        xn = sb("xn", [P, QT, D])
        cnt = sb("cnt", [P, QT * 2 * H, E], BF16)
        cmp_ = sb("cmp", [P, QT * 2 * H, E], BF16)
        gsum = sb("gsum", [P, QT * 2 * H])
        st = sb("st", [P, QT, 6])
        mv = sb("mv", [P, QT, 2])
        tick = sb("tick", [P, 1])
        ptick = sb("ptick", [P, 1])
        ve = sb("ve", [P, QT])
        rstd = sb("rstd", [P, QT])
        xT = sb("xT", [D, S])
        xhl = sb("xhl", [D, 2, S], F32R)
        gate = sb("gate", [P, QT, 2 * HE])
        gn = sb("gn", [P, 2, QT, E])
        nmin = sb("nmin", [P, 2, QT])
        den = sb("den", [P, 2, QT])
        rden = sb("rden", [P, 2, QT])
        base = ExitStack()
        with base:
            qhl = sb("qhl", [D, 2, S], F32R, base)
            chl = sb("chl", [P, 2, S], F32R, base)
            vv = sb("vv", [P, 2, QT, P], F32, base)
            pt = sb("pt", [P, QT, S], F32, base)
            pp = sb("pp", [P, 2, S], F32, base)
            vt = sb("vt", [P, 2, G * P], F32, base)
            ot = sb("ot", [P, 2, G * D], F32, base)
            acc = sb("acc", [P, QT, G * D], F32, base)
        base = ExitStack()
        with base:
            qk = sb("qk", [P, NG, 2, S], F32R, base)
            vext = sb("vext", [P, QT, NH, R // 2], F32, base)
            pm = sb("pm", [P, 2 * GH, S], F32, base)
            mmax = sb("mmax", [P, 2, QT, GH], F32, base)
            mrow = sb("mrow", [P, QT, GH, R], F32R, base)
            oT = sb("oT", [P, S], F32, base)
            oN = sb("oN", [P, QT, NH, DH], F32, base)
            mrd = sb("mrd", [P, QT, GH], F32, base)
        base = ExitStack()
        with base:
            raw = sb("raw", [P, 4, E, P], F32, base)
            qraw = sb("qraw", [P, H, D], F32, base)
            kraw = sb("kraw", [P, H, D], F32, base)
            wraw = sb("wraw", [P, 3, D], F32, base)
            woraw = sb("woraw", [P, D], F32, base)
            selraw = sb("selraw", [P, D], F32, base)
            braw = sb("braw", [1, 3 * D], F32, base)
            rsraw = sb("rsraw", [1, 1], F32, base)
            brow = sb("brow", [1, 2 * NG + 2, P], F32, base)
            bvrow = sb("bvrow", [1, NH * DH], F32, base)
            mf = sb("mf", [P, H, D], F32, base)

        bank = [ctx.enter_context(nc.psum_tensor(f"bank{i}", [P, 512], F32)) for i in range(8)]
        gb = bank[0:4]
        sbk = bank[4:6]
        tb = bank[6]
        qc = bank[7]
        kc = bank[5]

        x_first = sem("x_first")
        x_rest = sem("x_rest")
        small_in = sem("small_in")
        raw_free = sem("raw_free")
        ones_set = sem("ones_set")
        ident_set = sem("ident_set")
        pool_own = sem("pool_own")
        dve_own = sem("dve_own")
        act_own = sem("act_own")
        tr_small = sem("tr_small")
        mh_mm = sem("mh_mm")
        mh_scaled = sem("mh_scaled")
        setup_rows = sem("setup_rows")
        rows_mm = sem("rows_mm")
        sel_ready = sem("sel_ready")
        act_setup = sem("act_setup")
        mv_ready = sem("mv_ready")
        rstd_ready = sem("rstd_ready")
        xn_ready = sem("xn_ready")
        xt_mm = sem("xt_mm")
        xt_ready = sem("xt_ready")
        lg_mm = sem("lg_mm")
        lg_exp = sem("lg_exp")
        prep_done = sem("prep_done")
        gates_in = sem("gates_in")
        q_mm = sem("q_mm")
        q_hi = sem("q_hi")
        q_lo = sem("q_lo")
        s_mm = sem("s_mm")
        s_min = sem("s_min")
        s_exp = sem("s_exp")
        t_mm = sem("t_mm")
        pt_act = sem("pt_act")
        pt_dve = sem("pt_dve")
        av_mm = sem("av_mm")
        c_hi = sem("c_hi")
        c_lo = sem("c_lo")
        gn_ready = sem("gn_ready")
        v0_mm = sem("v0_mm")
        v1_mm = sem("v1_mm")
        o0_mm = sem("o0_mm")
        o1_mm = sem("o1_mm")
        v_act = sem("v_act")
        v_dve = sem("v_dve")
        o_act = sem("o_act")
        o_dve = sem("o_dve")
        v_fold = sem("v_fold")
        o_acc = sem("o_acc")
        x_ffn = sem("x_ffn")
        mv_mm = sem("mv_mm")
        vext_ready = sem("vext_ready")
        qk_mm = sem("qk_mm")
        qk_hi = sem("qk_hi")
        qk_masked = sem("qk_masked")
        qk_ready = sem("qk_ready")
        ms_mm = sem("ms_mm")
        m_max = sem("m_max")
        m_split = sem("m_split")
        m_tr = sem("m_tr")
        m_added = sem("m_added")
        mrow_set = sem("mrow_set")
        mb_mm = sem("mb_mm")
        m_exp = sem("m_exp")
        mav_mm = sem("mav_mm")
        ot_ready = sem("ot_ready")
        ott_mm = sem("ott_mm")
        on_ready = sem("on_ready")
        ont_mm = sem("ont_mm")
        ont_ready = sem("ont_ready")
        proj_mm = sem("proj_mm")
        x_mha = sem("x_mha")
        stored = sem("stored")
        experts_in = [sem(f"experts_in{i}") for i in range(4)]
        x_v = x.rearrange("b (t p) d -> p (b t) d", p=P)
        out_v = out.rearrange("b (t p) d -> p (b t) d", p=P)
        wv_v = v_w.rearrange("n d p -> d n p")
        wo_v = o_w.rearrange("n p d -> p n d")
        SMALL = 9 * 16

        block = ctx.enter_context(nc.Block())

        @block.sync
        def _(sp):
            sp.dma_start(xs[:, 0:QT, :], x_v[:, 0:QT, :]).then_inc(x_first, 16)
            sp.dma_start(selraw[0:HE, :], sel_v_w).then_inc(small_in, 16)
            sp.dma_start(selraw[HE:2 * HE, :], sel_o_w).then_inc(small_in, 16)
            sp.dma_start(qraw[:], q_w.rearrange("(h p) d -> p h d", p=P)).then_inc(small_in, 16)
            sp.dma_start(kraw[:], k_w.rearrange("(h p) d -> p h d", p=P)).then_inc(small_in, 16)
            sp.dma_start(wraw[:], W_qkv.rearrange("(t p) d -> p t d", p=P)).then_inc(small_in, 16)
            sp.dma_start(woraw[:], W_out).then_inc(small_in, 16)
            sp.dma_start(braw[:], b_qkv.rearrange("(a n) -> a n", a=1)).then_inc(small_in, 16)
            sp.dma_start(bout[:], b_out.rearrange("(a n) -> a n", a=1)).then_inc(small_in, 16)
            sp.dma_start(rsraw[:], route_scale.rearrange("(a n) -> a n", a=1)).then_inc(small_in, 16)
            for n in range(2 * H):
                if n >= 4:
                    sp.wait_ge(raw_free, n - 3)
                src = (wv_v, wo_v)[n % 2][:, (n // 2) * E:(n // 2 + 1) * E, :]
                sp.dma_start(raw[:, n % 4], src).then_inc(experts_in[n % 4], 16)
            sp.dma_start(xs[:, QT:, :], x_v[:, QT:, :]).then_inc(x_rest, 16)
            with sp.Fori(0, B) as b:
                sp.wait_ge(x_ffn, b + (B + 2))
                sp.dma_start(out_v[:, bass.ts(b, QT), :], xs[:, bass.ts(b, QT), :]).then_inc(stored, 16)
            sp.wait_ge(stored, 16 * B)

        @block.tensor
        def _(pe):
            mm, tr = nc.tensor.matmul, nc.tensor.transpose

            def split3(o, hi, lo, rhi, rlo):
                mm(o, hi, rhi, start=True, stop=False)
                mm(o, hi, rlo, start=False, stop=False)
                return mm(o, lo, rhi, start=False, stop=True)

            def prep_transpose(n, at=qc):
                pe.wait_ge(xn_ready, n + 1)
                for k in range(QT):
                    last = tr(at[:, k * P:(k + 1) * P], xn[:, k, :], ident[:])
                last.then_inc(xt_mm, 1)

            def prep_logits(n, at=qc):
                pe.wait_ge(xt_ready, n + 1)
                for k in range(QT):
                    last = mm(at[:, k * P:(k + 1) * P], xT[:, k * P:(k + 1) * P], selT[:], start=True, stop=True)
                last.then_inc(lg_mm, 1)

            pe.wait_ge(small_in, SMALL)
            pe.wait_ge(ident_set, 1)
            tr(bank[0][:, 0:P], selraw[:], ident[:])
            tr(bank[0][:, P:2 * P], woraw[:], ident[:]).then_inc(tr_small, 1)
            for t in range(3):
                last = tr(bank[1][:, t * P:(t + 1) * P], wraw[:, t, :], ident[:])
            last.then_inc(tr_small, 1)
            for h in range(H):
                last = mm(bank[2 + h // 4][:, (h % 4) * P:(h % 4 + 1) * P], qraw[:, h, :], kraw[:, h, :],
                          start=True, stop=True)
            last.then_inc(mh_mm, 1)
            pe.wait_ge(ones_set, 1)
            pe.wait_ge(setup_rows, 1)
            for c in range(2 * NG + 2):
                mm(bank[4][:, c:c + 1], brow[0:1, c, :], ones[0:1, 0:1], start=True, stop=True)
            mm(bank[5][:, 0:NH * DH], ones[0:1, :], bvrow[0:1, :], start=True, stop=True)
            mm(bank[5][:, P:P + 1], ones[0:1, :], rsraw[0:1, :], start=True, stop=True).then_inc(rows_mm, 1)
            prep_transpose(0)
            pe.wait_ge(sel_ready, 1)
            prep_logits(0)

            def ffn_steps(f, b, first):
                n = 4 * f + b
                t = 8 * f + b
                q, s_, u = 8 * n, UNITS * n, UNITS * n

                def query(h):
                    if h == 0:
                        pe.wait_ge(prep_done, n + 1 + f)
                    if h >= 2 or not first:
                        pe.wait_ge(c_lo, q + h - 1)
                    if h == 3:
                        pe.wait_ge(lg_exp, t + 2)
                    split3(qc[:], mh[:, 0, h, :], mh[:, 1, h, :], xhl[:, 0, :], xhl[:, 1, :]).then_inc(q_mm, 1)

                def score(h, k):
                    i = QT * h + k
                    if k == 0:
                        pe.wait_ge(q_lo, q + h + 1)
                    if i >= 2 or not first:
                        pe.wait_ge(s_exp, s_ + i - 1)
                    c = slice(k * P, (k + 1) * P)
                    split3(sbk[i % 2][:], qhl[:, 0, c], qhl[:, 1, c], xhl[:, 0, :], xhl[:, 1, :]).then_inc(s_mm, 1)

                def values(h, k, half):
                    i = QT * h + k
                    c = slice(k * P, (k + 1) * P)
                    done, free = ((v0_mm, v_act), (v1_mm, v_dve))[half]
                    if i >= 1 or not first:
                        pe.wait_ge(free, u + i)
                    e = slice(h * E + half * G, h * E + (half + 1) * G)
                    split3(gb[half][:], xhl[:, 0, c], xhl[:, 1, c], wv[:, 0, e, :], wv[:, 1, e, :]).then_inc(done, 1)

                def transposes(h, k):
                    i = QT * h + k
                    pe.wait_ge(s_exp, s_ + i + 1)
                    if i >= 1 or not first:
                        pe.wait_ge((pt_dve, pt_act)[(i - 1) % 2], 16 * n + (i - 1) // 2 + 1)
                    for c in range(QT):
                        last = tr(tb[:, c * P:(c + 1) * P], pp[:, i % 2, c * P:(c + 1) * P], ident[:])
                    last.then_inc(t_mm, 1)

                def context(h, shared):
                    pe.wait_ge(pt_act, 16 * n + 2 * h + 2)
                    pe.wait_ge(pt_dve, 16 * n + 2 * h + 2)
                    pe.wait_ge(v_fold, u + QT * (h + 1))
                    if shared:
                        pe.wait_ge(q_lo, q + h + 2)
                    for c in range(QT):
                        last = mm(qc[:], vv[:, h % 2, c, :], pt[:, c, :], start=(c == 0), stop=(c == QT - 1))
                    last.then_inc(av_mm, 1)

                def outputs(h, k, half):
                    i = QT * h + k
                    c = slice(k * P, (k + 1) * P)
                    done, free = ((o0_mm, o_act), (o1_mm, o_dve))[half]
                    if k == 0 and half == 0:
                        pe.wait_ge(c_lo, q + h + 1)
                    if i >= 1 or not first:
                        pe.wait_ge(free, u + i)
                    e = slice(h * E + half * G, h * E + (half + 1) * G)
                    split3(gb[2 + half][:], chl[:, 0, c], chl[:, 1, c], wo[:, 0, e, :], wo[:, 1, e, :]).then_inc(done, 1)

                return query, score, values, transposes, context, outputs

            def ffn_begin(f):
                query, _, values, _, _, _ = ffn_steps(f, 0, True)
                if f == 1:
                    pe.wait_ge(x_mha, B + 1)
                query(0)
                for k in range(QT):
                    values(0, k, 0)
                    values(0, k, 1)

            def ffn_stage(f, b, first, last):
                t, q = 8 * f + b, 8 * (4 * f + b)
                query, score, values, transposes, context, outputs = ffn_steps(f, b, first)
                if not last:
                    next_query, _, next_values, _, _, _ = ffn_steps(f, b + 1, False)
                for h in range(H):
                    more, past = h < H - 1, h >= 1
                    for k in range(QT):
                        if more:
                            values(h + 1, k, 0)
                        if past and k > 0:
                            outputs(h - 1, k, 0)
                        score(h, k)
                        if more and k == QT - 1:
                            query(h + 1)
                        if k >= 1:
                            transposes(h, k - 1)
                        if more:
                            values(h + 1, k, 1)
                        if past and k == 0:
                            outputs(h - 1, k, 0)
                        if k == QT - 1 and more:
                            transposes(h, k)
                        if past:
                            outputs(h - 1, k, 1)
                        if (h, k) == (2, 0):
                            pe.wait_ge(c_lo, q + 2)
                            prep_transpose(t + 1)
                        if (h, k) == (2, 1):
                            prep_logits(t + 1)
                    if more:
                        context(h, True)
                if not last:
                    next_query(0)
                transposes(H - 1, QT - 1)
                if not last:
                    next_values(0, 0, 0)
                    next_values(0, 0, 1)
                context(H - 1, not last)
                for k in range(QT):
                    if not last and k < QT - 1:
                        next_values(0, k + 1, 0)
                        next_values(0, k + 1, 1)
                    outputs(H - 1, k, 0)
                    outputs(H - 1, k, 1)

            def mha_steps(b, first):
                t = B + b
                m = MU * b

                def free(what):
                    at = PLACE[what] - 3
                    if at < 0 and first:
                        return
                    kind, i = FLOW[at]
                    if kind == "output" and first:
                        kind, i = FLOW[at - 3]
                    if kind == "score":
                        pe.wait_ge(m_max, m + i + 1 - (MU if at < 0 else 0))
                    elif kind == "values":
                        pe.wait_ge(vext_ready, b + 1)
                    else:
                        pe.wait_ge(x_mha, b + 1)

                def stack(g):
                    if g == 0:
                        pe.wait_ge(xt_ready, t + 1)
                    if g >= 1:
                        pe.wait_ge(qk_ready, 2 * NG * b + 2 * g)
                    if g == 0 and not first:
                        pe.wait_ge(m_added, NG * b - 1)
                        pe.wait_ge(on_ready, NG * b - 3)
                    if g == 1 and not first:
                        pe.wait_ge(m_added, NG * b)
                        pe.wait_ge(on_ready, NG * b - 2)
                    if g >= 2:
                        pe.wait_ge(m_added, NG * b + g - 1)
                    if g == 2 and not first:
                        pe.wait_ge(on_ready, NG * b - 1)
                    if g == 3 and not first:
                        pe.wait_ge(ont_ready, b)
                    mm(qc[:], wqs[:, g, :], xT[:], start=True, stop=True).then_inc(qk_mm, 1)
                    mm(kc[:], wks[:, g, :], xT[:], start=True, stop=True).then_inc(qk_mm, 1)

                def value_product():
                    free(("values", 0))
                    o = bank[PLACE["values", 0] % 3]
                    for k in range(QT):
                        last = mm(o[:, k * P:(k + 1) * P], xT[:, k * P:(k + 1) * P], wvT[:], start=True, stop=True)
                    last.then_inc(mv_mm, 1)

                def score(i):
                    g, k, j = i // GU, i // GH % QT, i % GH
                    if i % GU == 0:
                        pe.wait_ge(qk_ready, 2 * NG * b + 2 * g + 2)
                    free(("score", i))
                    r = slice(R * j, R * j + R)
                    mm(bank[PLACE["score", i] % 3][:], qk[r, g, 0, k * P:(k + 1) * P], qk[r, g, 1, :],
                       start=True, stop=True).then_inc(ms_mm, 1)

                def maxima(g):
                    pe.wait_ge(m_split, NG * b + g + 1)
                    for k in range(QT):
                        last = tr(kc[:, k * P:(k + 1) * P],
                                  mrow[:, k, :, :].rearrange("p j r -> p (j r)").bitcast(F32), ident[:])
                    last.then_inc(m_tr, 1)

                def score_t(i):
                    g, c, j = i // GU, i // GH % QT, i % GH
                    if i % GU == 0:
                        pe.wait_ge(m_added, NG * b + g + 1)
                    if i >= 2 or not first:
                        pe.wait_ge(m_exp, m + i - 1)
                    r = slice(R * j, R * j + R)
                    mm(bank[3 + i % 2][:], qk[r, g, 1, c * P:(c + 1) * P], qk[r, g, 0, :],
                       start=True, stop=True).then_inc(mb_mm, 1)

                def context(a):
                    g, c = a // QT, a % QT
                    pe.wait_ge(m_exp, m + GH * (a + 1))
                    if c == 0 and g == 0:
                        pe.wait_ge(vext_ready, b + 1)
                    if c == 0 and (g >= 1 or not first):
                        pe.wait_ge(ot_ready, NG * b + g)
                    for j in range(GH):
                        last = mm(tb[R * j:R * j + R // 2, :], vext[:, c, GH * g + j, :], pm[:, (GH * a + j) % (2 * GH), :],
                                  start=(c == 0), stop=(c == QT - 1), skip_group_check=True)
                    last.then_inc(mav_mm, 1)

                def out_transposes(g):
                    pe.wait_ge(ot_ready, NG * b + g + 1)
                    if g >= 1 or not first:
                        pe.wait_ge(on_ready, NG * b + g)
                    for k in range(QT):
                        last = tr(qc[:, k * P:(k + 1) * P], oT[:, k * P:(k + 1) * P], ident[:])
                    last.then_inc(ott_mm, 1)

                def output_transposes():
                    pe.wait_ge(on_ready, NG * b + NG)
                    for k in range(QT):
                        last = tr(qc[:, k * P:(k + 1) * P], oN[:, k, :, :].rearrange("p h d -> p (h d)"), ident[:])
                    last.then_inc(ont_mm, 1)

                def output_product(wait):
                    wait()
                    pe.wait_ge(ont_ready, b + 1)
                    for k in range(QT):
                        o = bank[PLACE["output", 0] % 3][:, k * P:(k + 1) * P]
                        mm(o, oT[:, k * P:(k + 1) * P], woT[:], start=True, stop=False)
                        last = mm(o, ones[0:1, :], bout[0:1, :], start=False, stop=True)
                    last.then_inc(proj_mm, 1)

                return (free, stack, value_product, score, maxima, score_t, context, out_transposes,
                        output_transposes, output_product)

            def mha_finish(prev, s, alone, next_qk):
                b = prev[-1]
                _, _, _, _, maxima, score_t, context, out_transposes, output_transposes, output_product = prev[:-1]
                i = s - LAG + MU
                if i < MU:
                    score_t(i)
                if i % GH == 2 and i < MU + GH:
                    context(i // GH - 1)
                if s == 3:
                    if not alone:
                        pe.wait_ge(qk_ready, next_qk + 2)
                    maxima(NG - 1)
                if s in (0, 16, 32):
                    if not alone:
                        pe.wait_ge(qk_ready, next_qk + 2 + s // 8)
                    out_transposes(1 + s // 16)
                if s == 36:
                    output_transposes()

            def mha_stage(b, first, last):
                t, m = B + b, MU * b
                steps = mha_steps(b, first)
                free, stack, value_product, score, maxima, score_t, context, out_transposes, _, _ = steps
                if not last:
                    next_stack = mha_steps(b + 1, False)[1]
                if not first:
                    prev = mha_steps(b - 1, False) + (b - 1,)
                for s in range(MU):
                    g, w = s // GU, s % GU
                    i = s - LAG
                    if s == V_STEP:
                        value_product()
                    if s == PROJ_STEP and not first:
                        prev[-2](lambda: free(("output", 0)))
                    score(s)
                    if not first:
                        mha_finish(prev, s, False, 2 * NG * b)
                    if i >= 0:
                        score_t(i)
                    if i >= GH and i % GH == 2:
                        context(i // GH - 1)
                    if g < NG - 1 and w == 8:
                        stack(g + 1)
                    if g in (1, 2) and w == 3:
                        pe.wait_ge(qk_ready, 2 * NG * b + 2 * g + 2)
                        maxima(g - 1)
                    if s == 44:
                        pe.wait_ge(qk_ready, 2 * NG * (b + 1))
                        prep_transpose(t + 1, kc)
                    if s == 48:
                        prep_logits(t + 1, kc)
                        pe.wait_ge(qk_ready, 2 * NG * (b + 1))
                        out_transposes(0)
                    if s == 51:
                        pe.wait_ge(lg_exp, t + 2)
                        maxima(2)
                    if s == 56 and not last:
                        next_stack(0)

            ffn_begin(0)
            ffn_stage(0, 0, True, False)
            with pe.Fori(1, B - 1) as b:
                ffn_stage(0, b, False, False)
            ffn_stage(0, B - 1, False, True)
            pe.wait_ge(x_ffn, B + 1)
            mha_steps(0, True)[1](0)
            mha_stage(0, True, False)
            with pe.Fori(1, B - 1) as b:
                mha_stage(b, False, False)
            mha_stage(B - 1, False, True)
            finish = mha_steps(B - 1, False) + (B - 1,)
            for s in range(TAIL):
                if s == PROJ_STEP:
                    finish[-2](lambda: pe.wait_ge(m_max, MU * B))
                mha_finish(finish, s, True, 0)
            ffn_begin(1)
            ffn_stage(1, 0, True, False)
            with pe.Fori(1, B - 1) as b:
                ffn_stage(1, b, False, False)
            ffn_stage(1, B - 1, False, True)

        @block.scalar
        def _(act):
            activation = nc.scalar.activation

            def prep(n, at=qc):
                act.wait_ge(xt_mm, n + 1)
                activation(xT[:], at[:], ACT.Copy).then_inc(xt_ready, 1)

            def prep_exp(n, at=qc):
                act.wait_ge(lg_mm, n + 1)
                activation(xn[:].rearrange("p t d -> p (t d)"), at[:], ACT.Exp, scale=-1.0).then_inc(lg_exp, 1)

            act.wait_ge(mh_mm, 1)
            for h in range(2):
                last = activation(mf[:, 4 * h:4 * h + 4, :].rearrange("p h d -> p (h d)"), bank[2 + h][:], ACT.Copy,
                                  scale=-FFN_SCALE)
            last.then_inc(mh_scaled, 1)
            prep(0)
            prep_exp(0)
            for n in range(2 * H):
                act.wait_ge(experts_in[n % 4], 16 * (n // 4 + 1))
                w = (wv, wo)[n % 2]
                h = n // 2
                activation(w[:, 0, h * E:(h + 1) * E, :], raw[:, n % 4], ACT.Copy).then_inc(act_setup, 1)

            def ffn_steps(f, b, first):
                n = 4 * f + b
                t = 8 * f + b
                q, u = 8 * n, UNITS * n

                def query(h):
                    act.wait_ge(q_mm, q + h + 1)
                    activation(qhl[:, 0, :], qc[:], ACT.Copy).then_inc(q_hi, 1)

                def context(h):
                    act.wait_ge(av_mm, q + h + 1)
                    activation(chl[:, 0, :], qc[:], ACT.Copy).then_inc(c_hi, 1)

                def values(h, k):
                    i = QT * h + k
                    act.wait_ge(v0_mm, u + i + 1)
                    if i == 0:
                        act.wait_ge(gates_in, n + 1 + f)
                    if i >= 2 or not first:
                        act.wait_ge(v_fold, u + i - 1)
                    for e in range(G):
                        last = activation(vt[:, i % 2, e * P:(e + 1) * P], gb[0][:, e * P:(e + 1) * P], ACT.Copy,
                                          scale=gate[:, k, h * E + e:h * E + e + 1])
                    last.then_inc(v_act, 1)

                def softmax(h, k):
                    i = QT * h + k
                    act.wait_ge(s_min, u + i + 1)
                    if i >= 2 or not first:
                        act.wait_ge(t_mm, u + i - 1)
                    activation(pp[:, i % 2, :], sbk[i % 2][:], ACT.Exp, bias=nmin[:, h % 2, k:k + 1], scale=-1.0,
                               accum_out=den[:, h % 2, k:k + 1]).then_inc(s_exp, 1)

                def copy_pt(h, k):
                    i = QT * h + k
                    act.wait_ge(t_mm, u + i + 1)
                    if k == 1 and (h >= 1 or not first):
                        act.wait_ge(av_mm, q + h)
                    activation(pt[:, :, k * P:(k + 1) * P], tb[:].rearrange("p (c q) -> p c q", c=QT),
                               ACT.Copy).then_inc(pt_act, 1)

                def outputs(h, k):
                    i = QT * h + k
                    act.wait_ge(o0_mm, u + i + 1)
                    if k == 0:
                        act.wait_ge(gn_ready, q + h + 1)
                    if i == 0:
                        act.wait_ge(x_ffn, n + 1)
                    if h >= 1 and i - QT >= 2:
                        act.wait_ge(o_acc, (UNITS - QT) * n + i - QT - 1)
                    o = acc[:, k, :] if h == 0 else ot[:, i % 2, :]
                    for e in range(G):
                        last = activation(o[:, e * D:(e + 1) * D], gb[2][:, e * D:(e + 1) * D], ACT.Copy,
                                          scale=gn[:, h % 2, k, e:e + 1])
                    last.then_inc(o_act, 1)

                return query, context, values, softmax, copy_pt, outputs

            def ffn_begin(f):
                query, _, values, _, _, _ = ffn_steps(f, 0, True)
                if f == 1:
                    act.wait_ge(x_mha, B + 1)
                query(0)
                for k in range(QT):
                    values(0, k)

            def ffn_stage(f, b, first, last):
                t = 8 * f + b
                query, context, values, softmax, copy_pt, outputs = ffn_steps(f, b, first)
                if not last:
                    next_query, _, next_values, _, _, _ = ffn_steps(f, b + 1, False)
                for h in range(H):
                    more, past = h < H - 1, h >= 1
                    for k in range(QT):
                        if more:
                            values(h + 1, k)
                        if past and k > 0:
                            outputs(h - 1, k)
                        softmax(h, k)
                        if more and k == QT - 1:
                            query(h + 1)
                        if past and k == 0:
                            outputs(h - 1, k)
                        if k == 2:
                            copy_pt(h, 1)
                        if (h, k) == (2, 0):
                            prep(t + 1)
                        if (h, k) == (2, 2):
                            prep_exp(t + 1)
                    if more:
                        copy_pt(h, QT - 1)
                        context(h)
                if not last:
                    next_query(0)
                copy_pt(H - 1, QT - 1)
                if not last:
                    next_values(0, 0)
                context(H - 1)
                for k in range(QT):
                    if not last and k < QT - 1:
                        next_values(0, k + 1)
                    outputs(H - 1, k)

            def mha_steps(b, first):
                m = MU * b

                def stack(g):
                    if not first:
                        act.wait_ge(mb_mm, m - MU + GU * (g + 1))
                    for c in range(2):
                        act.wait_ge(qk_mm, 2 * NG * b + 2 * g + c + 1)
                        activation(qk[:, g, c, :], (qc, kc)[c][:], ACT.Identity,
                                   bias=bst[:, c * NG + g:c * NG + g + 1]).then_inc(qk_hi, 1)

                def softmax(i):
                    act.wait_ge(mb_mm, m + i + 1)
                    if i >= 2 * GH or not first:
                        act.wait_ge(mav_mm, QT * NG * b + i // GH - 1)
                    activation(pm[:, i % (2 * GH), :], bank[3 + i % 2][:], ACT.Exp).then_inc(m_exp, 1)

                def copy_out(g):
                    act.wait_ge(mav_mm, QT * NG * b + QT * (g + 1))
                    if g >= 1:
                        act.wait_ge(ott_mm, NG * b + g)
                    elif not first:
                        act.wait_ge(proj_mm, b)
                    activation(oT[:], tb[:], ACT.Copy).then_inc(ot_ready, 1)

                def copy_output():
                    act.wait_ge(ont_mm, b + 1)
                    activation(oT[:], qc[:], ACT.Copy).then_inc(ont_ready, 1)

                return stack, softmax, copy_out, copy_output

            def mha_finish(prev, s):
                _, softmax, copy_out, copy_output = prev
                if s < LAG:
                    softmax(MU + s - LAG)
                if s in (14, 30):
                    copy_out(2 + s // 16)
                if s == 37:
                    copy_output()

            def mha_stage(b, first, last):
                t = B + b
                stack, softmax, copy_out, _ = mha_steps(b, first)
                for s in range(MU):
                    g, w = s // GU, s % GU
                    if not first:
                        mha_finish(mha_steps(b - 1, False), s)
                    if s >= LAG:
                        softmax(s - LAG)
                    if g < NG - 1 and w == 9:
                        stack(g + 1)
                    if s in (46, 62):
                        copy_out(s // 16 - 2)
                    if s == 45:
                        prep(t + 1, kc)
                    if s == 49:
                        prep_exp(t + 1, kc)
                    if s == 57 and not last:
                        mha_steps(b + 1, False)[0](0)

            ffn_begin(0)
            ffn_stage(0, 0, True, False)
            with act.Fori(1, B - 1) as b:
                ffn_stage(0, b, False, False)
            ffn_stage(0, B - 1, False, True)
            act.wait_ge(x_ffn, B + 1)
            mha_steps(0, True)[0](0)
            mha_stage(0, True, False)
            with act.Fori(1, B - 1) as b:
                mha_stage(b, False, False)
            mha_stage(B - 1, False, True)
            for s in range(TAIL):
                mha_finish(mha_steps(B - 1, False), s)
            ffn_begin(1)
            ffn_stage(1, 0, True, False)
            with act.Fori(1, B - 1) as b:
                ffn_stage(1, b, False, False)
            ffn_stage(1, B - 1, False, True)

        @block.vector
        def _(dve):
            v = nc.vector
            own = Chain(dve, dve_own)
            PREP = 13 + 3 * (E - 1)
            FFN_OWN = PREP + H
            MHA_OWN = 2 * NG + 1
            M = QT * 2 * H
            pr = xn[:].rearrange("p t (g e) -> p (t g) e", e=E)

            def statistics(nb):
                for k in range(QT):
                    last = v.bn_stats(st[:, k, :], xs[:, nb * QT + k, :])
                own.link(last)
                v.memset(tick[:], 0.0)
                for k in range(QT):
                    last = v.bn_aggr(mv[:, k, :], st[:, k, :])
                last.then_inc(mv_ready, 1)

            def normalise(n, nb):
                dve.wait_ge(rstd_ready, n + 1)
                for k in range(QT):
                    last = v.tensor_scalar(xn[:, k, :], xs[:, nb * QT + k, :], mv[:, k, 0:1], rstd[:, k:k + 1],
                                           ALU.subtract, ALU.mult)
                last.then_inc(xn_ready, 1)

            def denominators(n):
                dve.wait_ge(lg_exp, n + 1)
                own.link(v.memset(cnt[:], 0.0))
                own.link(v.tensor_scalar_add(pr, pr, 1.0))

            def sigmoids(half):
                o = xn[:, half * QT // 2:(half + 1) * QT // 2, :]
                own.link(v.reciprocal(o, o))

            def ranks(*distances):
                for k in distances:
                    own.link(v.tensor_tensor(cmp_[:, :, 0:E - k], pr[:, :, 0:E - k], pr[:, :, k:E], ALU.is_ge))
                    own.link(v.tensor_tensor(cnt[:, :, k:E], cnt[:, :, k:E], cmp_[:, :, 0:E - k], ALU.add))
                    own.link(v.tensor_tensor(cnt[:, :, 0:E - k], cnt[:, :, 0:E - k], cmp_[:, :, 0:E - k], ALU.subtract))

            def mask_best():
                return v.tensor_tensor(cmp_[:], cnt[:], thr[:].unsqueeze(1).to_broadcast([P, M, E]), ALU.is_lt)

            def choose():
                own.link(v.tensor_tensor(pr, pr, cmp_[:], ALU.mult))
                own.link(v.tensor_reduce(gsum[:], pr, AX.X, ALU.add))

            def over_sum():
                own.link(v.tensor_scalar_max(gsum[:], gsum[:], 1e-9))
                own.link(v.reciprocal(gsum[:], gsum[:]))
                own.link(v.tensor_tensor(gsum[:].rearrange("p (t g) -> p t g", t=QT),
                                         gsum[:].rearrange("p (t g) -> p t g", t=QT),
                                         rsb[:].unsqueeze(1).to_broadcast([P, QT, 2 * H]), ALU.mult))

            def weights():
                own.link(v.tensor_tensor(pr, pr, gsum[:].unsqueeze(2).to_broadcast([P, M, E]), ALU.mult))

            def gates(n):
                denominators(n)
                sigmoids(0)
                sigmoids(1)
                ranks(*range(1, E))
                own.link(mask_best())
                choose()
                over_sum()
                weights()

            def commit_x():
                own.link(v.tensor_copy(xhl[:, 0, :], xT[:]))
                v.tensor_tensor(xhl[:, 1, :], xT[:], xhl[:, 0, :].bitcast(F32), ALU.subtract).then_inc(prep_done, 1)

            def commit_gates():
                v.tensor_copy(gate[:].rearrange("p t d -> p (t d)"), xn[:].rearrange("p t d -> p (t d)"))\
                    .then_inc(gates_in, 1)

            v.memset(ones[:], 1.0)
            v.memset(ph[:], -0.5)
            v.memset(eps[:], LN_EPS)
            v.memset(wqs[:], 0.0)
            v.memset(wks[:], 0.0)
            for e in range(E):
                v.memset(thr[:, e:e + 1], float(e - (E - 3)))
            own.link(v.memset(brow[:], 0.0))
            v.tensor_copy(ones[:], ones[:]).then_inc(ones_set, 1)
            v.memset(gsum[:], 0.0).then_inc(x_mha, 1)
            dve.wait_ge(x_first, 16)
            statistics(0)
            normalise(0, 0)
            dve.wait_ge(small_in, SMALL)
            heads = braw[:].rearrange("p (h c) -> p h c", h=NH)
            for r in range(3):
                c = slice(DH * r, DH * r + DH)
                v.tensor_scalar_mul(brow[0:1, 0:NG, :].rearrange("p g (j r) -> p (g j) r", j=GH)[:, :, c],
                                    heads[:, :, 0:DH], MHA_SCALE)
                v.tensor_copy(brow[0:1, NG:2 * NG, :].rearrange("p g (j r) -> p (g j) r", j=GH)[:, :, c],
                              heads[:, :, DH:2 * DH])
            v.memset(brow[0:1, NG:2 * NG, :].rearrange("p g (j r) -> p (g j) r", j=GH)[:, :, 3 * DH:3 * DH + 2], -1.0)
            v.memset(brow[0:1, 2 * NG, :].rearrange("p (j r) -> p j r", j=GH)[:, :, 2 * DH:3 * DH], -1.0)
            v.memset(brow[0:1, 2 * NG + 1, :].rearrange("p (j r) -> p j r", j=GH)[:, :, DH:2 * DH], -1.0)
            v.tensor_copy(bvrow[:].rearrange("p (h c) -> p h c", h=NH), heads[:, :, 2 * DH:3 * DH]).then_inc(setup_rows, 1)
            dve.wait_ge(tr_small, 2)
            v.tensor_copy(selT[:], bank[0][:, 0:P]).then_inc(sel_ready, 1)
            v.tensor_copy(woT[:], bank[0][:, P:2 * P])
            wh = bank[1][:, 0:3 * P].rearrange("p (h c) -> p h c", h=NH)
            for r in range(3):
                c = slice(DH * r, DH * r + DH)
                v.tensor_scalar_mul(wqs[:].rearrange("p g (j r) -> p (g j) r", j=GH)[:, :, c], wh[:, :, 0:DH], MHA_SCALE)
                v.tensor_copy(wks[:].rearrange("p g (j r) -> p (g j) r", j=GH)[:, :, c], wh[:, :, DH:2 * DH])
            v.tensor_copy(wvT[:].rearrange("p (h c) -> p h c", h=NH), wh[:, :, 2 * DH:3 * DH])
            dve.wait_ge(rows_mm, 1)
            v.tensor_copy(bst[:], bank[4][:, 0:2 * NG + 2])
            v.tensor_copy(bvb[:], bank[5][:, 0:NH * DH])
            v.tensor_copy(rsb[:, 0:H], bank[5][:, P:P + 1].to_broadcast([P, H]))
            own.link(v.tensor_scalar_mul(rsb[:, H:2 * H], bank[5][:, P:P + 1].to_broadcast([P, H]), 0.5))
            dve.wait_ge(mh_scaled, 1)
            own.link(v.tensor_copy(mh[:, 0, :, :], mf[:]))
            v.tensor_tensor(mh[:, 1, :, :], mf[:], mh[:, 0, :, :].bitcast(F32), ALU.subtract)
            gates(0)
            for n in range(2 * H):
                w = (wv, wo)[n % 2]
                h = n // 2
                dve.wait_ge(act_setup, n + 1)
                v.tensor_tensor(w[:, 1, h * E:(h + 1) * E, :], raw[:, n % 4],
                                w[:, 0, h * E:(h + 1) * E, :].bitcast(F32), ALU.subtract).then_inc(raw_free, 1)
            commit_x()
            commit_gates()
            dve.wait_ge(x_rest, 16)

            def ffn_steps(f, b, first):
                n = 4 * f + b
                t = 8 * f + b
                q, u = 8 * n, UNITS * n
                nb = (b + 1) % B

                def query(h):
                    dve.wait_ge(q_hi, q + h + 1)
                    v.tensor_tensor(qhl[:, 1, :], qc[:], qhl[:, 0, :].bitcast(F32), ALU.subtract).then_inc(q_lo, 1)

                def context(h):
                    dve.wait_ge(c_hi, q + h + 1)
                    v.tensor_tensor(chl[:, 1, :], qc[:], chl[:, 0, :].bitcast(F32), ALU.subtract).then_inc(c_lo, 1)

                def row_max(h, k):
                    i = QT * h + k
                    dve.wait_ge(s_mm, u + i + 1)
                    v.tensor_reduce(nmin[:, h % 2, k:k + 1], sbk[i % 2][:], AX.X, ALU.min).then_inc(s_min, 1)

                def values(h, k):
                    i = QT * h + k
                    dve.wait_ge(v1_mm, u + i + 1)
                    dve.wait_ge(v_act, u + i + 1)
                    for e in range(G):
                        o = vt[:, i % 2, e * P:(e + 1) * P]
                        last = v.scalar_tensor_tensor(o, gb[1][:, e * P:(e + 1) * P],
                                                      gate[:, k, h * E + G + e:h * E + G + e + 1], o, ALU.mult, ALU.add)
                    last.then_inc(v_dve, 1)

                def outputs(h, k):
                    i = QT * h + k
                    dve.wait_ge(o1_mm, u + i + 1)
                    dve.wait_ge(o_act, u + i + 1)
                    if k == 0:
                        dve.wait_ge(gn_ready, q + h + 1)
                    row = acc[:, k, :] if h == 0 else ot[:, i % 2, :]
                    for e in range(G):
                        o = row[:, e * D:(e + 1) * D]
                        last = v.scalar_tensor_tensor(o, gb[3][:, e * D:(e + 1) * D],
                                                      gn[:, h % 2, k, G + e:G + e + 1], o, ALU.mult, ALU.add)
                    last.then_inc(o_dve, 1)

                def copy_pt(h, k):
                    i = QT * h + k
                    dve.wait_ge(t_mm, u + i + 1)
                    if k == 0 and (h >= 1 or not first):
                        dve.wait_ge(av_mm, q + h)
                    v.tensor_copy(pt[:, :, k * P:(k + 1) * P], tb[:].rearrange("p (c q) -> p c q", c=QT))\
                        .then_inc(pt_dve, 1)

                def output_gates(h):
                    dve.wait_ge(s_exp, u + QT * (h + 1))
                    own.link(v.reciprocal(rden[:, h % 2, :], den[:, h % 2, :]))
                    v.tensor_tensor(gn[:, h % 2, :, :], gate[:, :, HE + h * E:HE + (h + 1) * E],
                                             rden[:, h % 2, :].unsqueeze(2).to_broadcast([P, QT, E]), ALU.mult)\
                        .then_inc(gn_ready, 1)

                return query, context, row_max, values, outputs, copy_pt, output_gates

            def ffn_begin(f):
                query, _, _, values, _, _, _ = ffn_steps(f, 0, True)
                query(0)
                for k in range(QT):
                    values(0, k)

            def ffn_stage(f, b, first, last):
                n, t = 4 * f + b, 8 * f + b
                q, nb = 8 * n, (b + 1) % B
                query, context, row_max, values, outputs, copy_pt, output_gates = ffn_steps(f, b, first)
                if not last:
                    next_query, _, _, next_values, _, _, _ = ffn_steps(f, b + 1, False)
                for h in range(H):
                    more, past = h < H - 1, h >= 1
                    for k in range(QT):
                        row_max(h, k)
                        if h == H - 1 and k == QT - 1:
                            commit_x()
                        if k % 2 == 1:
                            copy_pt(h, k - 1)
                        if more and k == QT - 1:
                            query(h + 1)
                        if more:
                            values(h + 1, k)
                        if past:
                            outputs(h - 1, k)
                        if (h, k) == (1, 2):
                            dve.wait_ge(x_ffn, n + 1)
                            statistics(nb)
                        if (h, k) == (H - 1, 0):
                            choose()
                        if (h, k) == (H - 1, 1):
                            over_sum()
                        if (h, k) == (H - 1, 2):
                            weights()
                    if h == 1:
                        normalise(t + 1, nb)
                    if h == H - 1 and not last:
                        next_query(0)
                    output_gates(h)
                    if h == 2:
                        denominators(t + 1)
                    if h in (2, 3):
                        sigmoids(h - 2)
                    if h in (3, 4, 5, 6):
                        ranks(*((7,), (1, 2), (3, 4), (5, 6))[h - 3])
                    if h == H - 2:
                        own.link(mask_best())
                    if more:
                        context(h)
                dve.wait_ge(gn_ready, q + H)
                commit_gates()
                if not last:
                    next_values(0, 0)
                context(H - 1)
                for k in range(QT):
                    if not last and k < QT - 1:
                        next_values(0, k + 1)
                    outputs(H - 1, k)

            def mha_steps(b, first):
                m = MU * b

                def stack(g):
                    for c in range(2):
                        dve.wait_ge(qk_masked, 2 * NG * b + 2 * g + c + 1)
                        o = qk[:, g, c, :]
                        v.scalar_tensor_tensor(o, (qc, kc)[c][:], bst[:, c * NG + g:c * NG + g + 1], o.bitcast(F32),
                                               ALU.add, ALU.add).then_inc(qk_ready, 1)

                def values():
                    dve.wait_ge(mv_mm, b + 1)
                    if not first:
                        dve.wait_ge(mav_mm, QT * NG * b)
                    o = bank[PLACE["values", 0] % 3][:].rearrange("p (k h c) -> p k h c", k=QT, h=NH)
                    v.tensor_tensor(vext[:, :, :, 0:DH], o,
                                    bvb[:].rearrange("p (h c) -> p h c", h=NH).unsqueeze(1).to_broadcast([P, QT, NH, DH]),
                                    ALU.add).then_inc(vext_ready, 1)

                def row_max(i):
                    dve.wait_ge(ms_mm, m + i + 1)
                    if i % GU == 0 and (i >= 2 * GU or not first):
                        dve.wait_ge(m_split, NG * b + i // GU - 1)
                    v.tensor_reduce(mmax[:, i // GU % 2, i // GH % QT, i % GH:i % GH + 1],
                                    bank[PLACE["score", i] % 3][:], AX.X, ALU.max).then_inc(m_max, 1)

                def split_maxima(g):
                    dve.wait_ge(m_max, m + GU * (g + 1))
                    own.link(v.tensor_copy(mrow[:, :, :, 3 * DH], mmax[:, g % 2, :, :]))
                    v.tensor_tensor(mrow[:, :, :, 3 * DH + 1], mmax[:, g % 2, :, :],
                                    mrow[:, :, :, 3 * DH].bitcast(F32), ALU.subtract).then_inc(m_split, 1)

                def add_maxima(g):
                    dve.wait_ge(m_tr, NG * b + g + 1)
                    o = qk[:, g, 0, :]
                    v.tensor_tensor(o, o.bitcast(F32), kc[:], ALU.add).then_inc(m_added, 1)

                def over_sums(g):
                    dve.wait_ge(ott_mm, NG * b + g + 1)
                    if g == 0 and not first:
                        dve.wait_ge(ont_mm, b)
                    o = qc[:].rearrange("p (k j r) -> p k j r", k=QT, j=GH)
                    own.link(v.reciprocal(mrd[:], o[:, :, :, DH]))
                    v.tensor_tensor(oN[:, :, GH * g:GH * g + GH, :], o[:, :, :, 0:DH],
                                    mrd[:].unsqueeze(3).to_broadcast([P, QT, GH, DH]), ALU.mult).then_inc(on_ready, 1)

                def residual():
                    dve.wait_ge(proj_mm, b + 1)
                    xb = xs[:, bass.ts(b, QT), :]
                    o = bank[PLACE["output", 0] % 3][:].rearrange("p (k d) -> p k d", k=QT)
                    v.tensor_tensor(xb, xb, o, ALU.add).then_inc(x_mha, 1)

                return stack, values, row_max, split_maxima, add_maxima, over_sums, residual

            def mha_finish(prev, s):
                _, _, _, _, add_maxima, over_sums, residual = prev
                if s == 4:
                    add_maxima(NG - 1)
                if s in (2, 18, 34):
                    over_sums(1 + s // 16)
                if s == PROJ_STEP:
                    residual()

            def mha_stage(b, first, last):
                t, nb = B + b, (b + 1) % B
                stack, values, row_max, split_maxima, add_maxima, over_sums, _ = mha_steps(b, first)
                for s in range(MU):
                    g, w = s // GU, s % GU
                    if not first:
                        mha_finish(mha_steps(b - 1, False), s)
                    if s == V_STEP:
                        values()
                    row_max(s)
                    if g < NG - 1 and w == 11:
                        stack(g + 1)
                    if w == GU - 1:
                        if first and g == 0:
                            dve.wait_ge(mrow_set, 1)
                        split_maxima(g)
                    if g >= 1 and w == 4:
                        add_maxima(g - 1)
                    if s == 50:
                        over_sums(0)
                    if s == 12:
                        if last:
                            dve.wait_ge(x_mha, 2)
                        statistics(nb)
                    if s == 28:
                        dve.wait_ge(lg_exp, t + 1)
                        normalise(t + 1, nb)
                    if s == 59 and not last:
                        mha_steps(b + 1, False)[0](0)

            ffn_begin(0)
            ffn_stage(0, 0, True, False)
            with dve.Fori(1, B - 1) as b:
                own.enter(b - 1, FFN_OWN)
                ffn_stage(0, b, False, False)
            own.leave(B - 2)
            ffn_stage(0, B - 1, False, True)
            dve.wait_ge(x_ffn, B + 1)
            own.link(v.memset(vext[:, :, :, DH:DH + 1], 1.0))
            own.link(v.memset(vext[:, :, :, DH + 1:], 0.0))
            mha_steps(0, True)[0](0)
            mha_stage(0, True, False)
            with dve.Fori(1, B - 1) as b:
                own.enter(b - 1, MHA_OWN)
                mha_stage(b, False, False)
            own.leave(B - 2)
            mha_stage(B - 1, False, True)
            for s in range(TAIL):
                mha_finish(mha_steps(B - 1, False), s)
                if s == 5:
                    gates(2 * B)
            commit_x()
            commit_gates()
            ffn_begin(1)
            ffn_stage(1, 0, True, False)
            with dve.Fori(1, B - 1) as b:
                own.enter(b - 1, FFN_OWN)
                ffn_stage(1, b, False, False)
            own.leave(B - 2)
            ffn_stage(1, B - 1, False, True)

        @block.gpsimd
        def _(pool):
            g_ = nc.gpsimd
            own = Chain(pool, pool_own)
            PREP = 1

            def rstd_(n):
                pool.wait_ge(mv_ready, n + 1)
                own.link(g_.tensor_tensor(ve[:], mv[:, :, 1], eps[:], ALU.add))
                g_.tensor_tensor(rstd[:], ve[:], ph[:], ALU.pow).then_inc(rstd_ready, 1)

            own.link(g_.memset(ident[:], 0.0))
            g_.affine_select(out=ident[:], in_=ident[:], compare_op=ALU.not_equal, fill=1.0, base=0,
                             pattern=[[-1, P]], channel_multiplier=1).then_inc(ident_set, 1)
            g_.memset(ptick[:], 0.0).then_inc(x_ffn, 1)
            pool.wait_ge(ones_set, 1)
            rstd_(0)

            def ffn_steps(f, b, first):
                n = 4 * f + b
                u = UNITS * n

                def fold_values(h, k):
                    i = QT * h + k
                    pool.wait_ge(v_dve, u + i + 1)
                    a = vt[:, i % 2, :]
                    own.link(g_.tensor_tensor(a[:, 0:2 * P], a[:, 0:2 * P], a[:, 2 * P:4 * P], ALU.add))
                    if k == 0 and (h >= 2 or not first):
                        pool.wait_ge(av_mm, 8 * n + h - 1)
                    g_.tensor_tensor(vv[:, h % 2, k, :], a[:, 0:P], a[:, P:2 * P], ALU.add).then_inc(v_fold, 1)

                def add_outputs(h, k):
                    i = QT * h + k
                    pool.wait_ge(o_dve, u + i + 1)
                    g_.tensor_tensor(acc[:, k, :], acc[:, k, :], ot[:, i % 2, :], ALU.add).then_inc(o_acc, 1)

                return fold_values, add_outputs

            def ffn_begin(f):
                fold_values, _ = ffn_steps(f, 0, True)
                for k in range(QT):
                    fold_values(0, k)

            def fold_outputs(f, b):
                pool.wait_ge(o_acc, (UNITS - QT) * (4 * f + b + 1))
                own.link(g_.tensor_tensor(acc[:, :, 0:2 * D], acc[:, :, 0:2 * D], acc[:, :, 2 * D:4 * D], ALU.add))
                own.link(g_.tensor_tensor(acc[:, :, 0:D], acc[:, :, 0:D], acc[:, :, D:2 * D], ALU.add))
                xb = xs[:, bass.ts(b, QT), :]
                g_.tensor_tensor(xb, xb, acc[:, :, 0:D], ALU.add).then_inc(x_ffn, 1)

            def ffn_stage(f, b, first, last):
                t = 8 * f + b
                fold_values, add_outputs = ffn_steps(f, b, first)
                if not last:
                    next_fold, _ = ffn_steps(f, b + 1, False)
                for h in range(H):
                    for k in range(QT):
                        if h < H - 1:
                            fold_values(h + 1, k)
                        if h >= 2:
                            add_outputs(h - 1, k)
                    if h == 0 and not first:
                        fold_outputs(f, b - 1)
                    if h == 1:
                        rstd_(t + 1)
                if not last:
                    next_fold(0, 0)
                for k in range(QT):
                    if not last and k < QT - 1:
                        next_fold(0, k + 1)
                    add_outputs(H - 1, k)
                if last:
                    fold_outputs(f, b)

            FFN_OWN = UNITS + PREP + 2
            ffn_begin(0)
            ffn_stage(0, 0, True, False)
            with pool.Fori(1, B - 1) as b:
                own.enter(b - 1, FFN_OWN)
                ffn_stage(0, b, False, False)
            own.leave(B - 2)
            ffn_stage(0, B - 1, False, True)
            pool.wait_ge(x_ffn, B + 1)
            g_.memset(mrow[:].bitcast(F32), 0.0).then_inc(mrow_set, 1)

            def mask(b, g):
                for c in range(2):
                    pool.wait_ge(qk_hi, 2 * NG * b + 2 * g + c + 1)
                    o = qk[:, g, c, :]
                    g_.tensor_tensor(o, o.bitcast(F32), bst[:, 2 * NG + c:2 * NG + c + 1].to_broadcast([P, S]),
                                     ALU.mult).then_inc(qk_masked, 1)

            def mha_stage(b, last):
                mask(b, 1)
                rstd_(B + b + 1)
                mask(b, 2)
                mask(b, 3)
                if not last:
                    mask(b + 1, 0)

            mask(0, 0)
            mha_stage(0, False)
            with pool.Fori(1, B - 1) as b:
                own.enter(b - 1, PREP)
                mha_stage(b, False)
            own.leave(B - 2)
            mha_stage(B - 1, True)
            ffn_begin(1)
            ffn_stage(1, 0, True, False)
            with pool.Fori(1, B - 1) as b:
                own.enter(b - 1, FFN_OWN)
                ffn_stage(1, b, False, False)
            own.leave(B - 2)
            ffn_stage(1, B - 1, False, True)


_INS = ["L0_attn_x", "L0_attn_W_qkv", "L0_attn_b_qkv", "L0_attn_W_out", "L0_attn_b_out", "L0_ffn_q_w", "L0_ffn_k_w",
        "L0_ffn_v_w", "L0_ffn_o_w", "L0_ffn_sel_v_w", "L0_ffn_sel_o_w", "L0_ffn_route_scale"]


def kernel(**inputs):
    import concourse.bacc as bacc
    from concourse.bass_utils import run_bass_kernel_spmd

    nc = bacc.Bacc("TRN2", target_bir_lowering=False, num_devices=1)
    arrays, args = {}, []
    for name in _INS:
        a = np.ascontiguousarray(inputs[name])
        arrays[f"in_{name}"] = a
        args.append(nc.dram_tensor(f"in_{name}", a.shape, mybir.dt.from_np(a.dtype), kind="ExternalInput").ap())
    out = nc.dram_tensor("out_x", (B, S, D), F32, kind="ExternalOutput").ap()
    macaron_kernel(nc, *args, out)
    r = run_bass_kernel_spmd(nc, [arrays], core_ids=[0])
    return r.results[0]["out_x"]
```

```python
from contextlib import ExitStack

import numpy as np
import concourse.bass as bass
from concourse import mybir

F32 = mybir.dt.float32
F32R = mybir.dt.float32r
BF16 = mybir.dt.bfloat16
ALU = mybir.AluOpType
ACT = mybir.ActivationFunctionType
AX = mybir.AxisListType

B, S, D = 4, 512, 128
P = 128
QT = S // P
H, E = 8, 8
HE = H * E
G = 4
NH, DH = 16, 8
NG, GH = 4, 4
R = 32
LN_EPS = 1e-5
FFN_SCALE = 1.0 / float(np.sqrt(P))
MHA_SCALE = 1.0 / float(np.sqrt(DH))
UNITS = H * QT
GU = QT * GH
MU = NG * GU
LAG = 26
V_STEP, PROJ_STEP = 29, 39
TAIL = 41

FLOW = []
for _s in range(MU):
    FLOW += [("values", 0)] * (_s == V_STEP) + [("output", 0)] * (_s == PROJ_STEP) + [("score", _s)]
PLACE = {what: at for at, what in enumerate(FLOW)}
assert len(FLOW) % 3 == 0


class Chain:

    def __init__(self, eng, sem):
        self.eng, self.sem, self.done, self.base = eng, sem, 0, 0

    def then(self, ins):
        ins.then_inc(self.sem, 1)
        self.done += 1
        return ins

    def settle(self):
        self.eng.wait_ge(self.sem, self.base + self.done)

    def link(self, ins):
        self.then(ins)
        self.settle()

    def enter(self, i, per):
        self.before, self.per = self.done + 0, per
        self.base, self.done = i * per + self.before, 0

    def leave(self, trips):
        assert self.done == self.per, (self.done, self.per)
        self.base, self.done = 0, self.before + trips * self.per


def macaron_kernel(nc, x, W_qkv, b_qkv, W_out, b_out, q_w, k_w, v_w, o_w, sel_v_w, sel_o_w, route_scale, out):
    ctx = ExitStack()
    with ctx:
        def sb(name, shape, dt=F32, at=ctx):
            return at.enter_context(nc.sbuf_tensor(name, shape, dt))

        def sem(name):
            return ctx.enter_context(nc.semaphore(name))

        xs = sb("xs", [P, B * QT, D])
        wv = sb("wv", [P, 2, HE, P], F32R)
        wo = sb("wo", [P, 2, HE, D], F32R)
        mh = sb("mh", [P, 2, H, D], F32R)
        ident = sb("ident", [P, P])
        selT = sb("selT", [D, 2 * HE])
        wqs = sb("wqs", [D, NG, P])
        wks = sb("wks", [D, NG, P])
        wvT = sb("wvT", [D, NH * DH])
        woT = sb("woT", [NH * DH, D])
        bvb = sb("bvb", [P, NH * DH])
        bout = sb("bout", [1, D])
        bst = sb("bst", [P, 2 * NG + 2])
        ones = sb("ones", [1, P])
        thr = sb("thr", [P, E])
        rsb = sb("rsb", [P, 2 * H])
        ph = sb("ph", [P, QT])
        eps = sb("eps", [P, QT])
        xn = sb("xn", [P, QT, D])
        cnt = sb("cnt", [P, QT * 2 * H, E], BF16)
        cmp_ = sb("cmp", [P, QT * 2 * H, E], BF16)
        gsum = sb("gsum", [P, QT * 2 * H])
        st = sb("st", [P, QT, 6])
        mv = sb("mv", [P, QT, 2])
        tick = sb("tick", [P, 1])
        ptick = sb("ptick", [P, 1])
        ve = sb("ve", [P, QT])
        rstd = sb("rstd", [P, QT])
        xT = sb("xT", [D, S])
        xhl = sb("xhl", [D, 2, S], F32R)
        gate = sb("gate", [P, QT, 2 * HE])
        gn = sb("gn", [P, 2, QT, E])
        nmin = sb("nmin", [P, 2, QT])
        den = sb("den", [P, 2, QT])
        rden = sb("rden", [P, 2, QT])
        base = ExitStack()
        with base:
            qhl = sb("qhl", [D, 2, S], F32R, base)
            chl = sb("chl", [P, 2, S], F32R, base)
            vv = sb("vv", [P, 2, QT, P], F32, base)
            pt = sb("pt", [P, QT, S], F32, base)
            pp = sb("pp", [P, 2, S], F32, base)
            vt = sb("vt", [P, 2, G * P], F32, base)
            ot = sb("ot", [P, 2, G * D], F32, base)
            acc = sb("acc", [P, QT, G * D], F32, base)
        base = ExitStack()
        with base:
            qk = sb("qk", [P, NG, 2, S], F32R, base)
            vext = sb("vext", [P, QT, NH, R // 2], F32, base)
            pm = sb("pm", [P, 2 * GH, S], F32, base)
            mmax = sb("mmax", [P, 2, QT, GH], F32, base)
            mrow = sb("mrow", [P, QT, GH, R], F32R, base)
            oT = sb("oT", [P, S], F32, base)
            oN = sb("oN", [P, QT, NH, DH], F32, base)
            mrd = sb("mrd", [P, QT, GH], F32, base)
        base = ExitStack()
        with base:
            raw = sb("raw", [P, 4, E, P], F32, base)
            qraw = sb("qraw", [P, H, D], F32, base)
            kraw = sb("kraw", [P, H, D], F32, base)
            wraw = sb("wraw", [P, 3, D], F32, base)
            woraw = sb("woraw", [P, D], F32, base)
            selraw = sb("selraw", [P, D], F32, base)
            braw = sb("braw", [1, 3 * D], F32, base)
            rsraw = sb("rsraw", [1, 1], F32, base)
            brow = sb("brow", [1, 2 * NG + 2, P], F32, base)
            bvrow = sb("bvrow", [1, NH * DH], F32, base)
            mf = sb("mf", [P, H, D], F32, base)

        bank = [ctx.enter_context(nc.psum_tensor(f"bank{i}", [P, 512], F32)) for i in range(8)]
        gb = bank[0:4]
        sbk = bank[4:6]
        tb = bank[6]
        qc = bank[7]
        kc = bank[5]

        x_first = sem("x_first")
        x_rest = sem("x_rest")
        small_in = sem("small_in")
        raw_free = [sem(f"raw_free{i}") for i in range(4)]
        ones_set = sem("ones_set")
        ident_set = sem("ident_set")
        pool_own = sem("pool_own")
        dve_own = sem("dve_own")
        tr_small = sem("tr_small")
        mh_mm = sem("mh_mm")
        mh_scaled = sem("mh_scaled")
        setup_rows = sem("setup_rows")
        rows_mm = sem("rows_mm")
        sel_ready = sem("sel_ready")
        experts_hi = sem("experts_hi")
        mv_ready = sem("mv_ready")
        rstd_ready = sem("rstd_ready")
        xn_ready = sem("xn_ready")
        xt_mm = sem("xt_mm")
        xt_ready = sem("xt_ready")
        lg_mm = sem("lg_mm")
        lg_exp = sem("lg_exp")
        prep_done = sem("prep_done")
        gates_in = sem("gates_in")
        best_masked = sem("best_masked")
        best_picked = sem("best_picked")
        q_mm = sem("q_mm")
        q_hi = sem("q_hi")
        q_lo = sem("q_lo")
        s_mm = sem("s_mm")
        s_min = sem("s_min")
        s_exp = sem("s_exp")
        t_mm = sem("t_mm")
        pt_act = sem("pt_act")
        pt_dve = sem("pt_dve")
        av_mm = sem("av_mm")
        c_hi = sem("c_hi")
        c_lo = sem("c_lo")
        gn_ready = sem("gn_ready")
        v0_mm = sem("v0_mm")
        v1_mm = sem("v1_mm")
        o0_mm = sem("o0_mm")
        o1_mm = sem("o1_mm")
        v_act = sem("v_act")
        v_dve = sem("v_dve")
        o_act = sem("o_act")
        o_dve = sem("o_dve")
        v_fold = sem("v_fold")
        o_acc = sem("o_acc")
        x_ffn = sem("x_ffn")
        mv_mm = sem("mv_mm")
        vext_ready = sem("vext_ready")
        qk_mm = sem("qk_mm")
        qk_hi = sem("qk_hi")
        qk_masked = sem("qk_masked")
        qk_ready = sem("qk_ready")
        ms_mm = sem("ms_mm")
        m_max = sem("m_max")
        m_split = sem("m_split")
        m_tr = sem("m_tr")
        m_added = sem("m_added")
        mrow_set = sem("mrow_set")
        mb_mm = sem("mb_mm")
        m_exp = sem("m_exp")
        mav_mm = sem("mav_mm")
        ot_ready = sem("ot_ready")
        ott_mm = sem("ott_mm")
        on_ready = sem("on_ready")
        ont_mm = sem("ont_mm")
        ont_ready = sem("ont_ready")
        proj_mm = sem("proj_mm")
        x_mha = sem("x_mha")
        stored = sem("stored")
        experts_in = [sem(f"experts_in{i}") for i in range(4)]
        x_v = x.rearrange("b (t p) d -> p (b t) d", p=P)
        out_v = out.rearrange("b (t p) d -> p (b t) d", p=P)
        wv_v = v_w.rearrange("n d p -> d n p")
        wo_v = o_w.rearrange("n p d -> p n d")
        SMALL = 9 * 16

        block = ctx.enter_context(nc.Block())

        @block.sync
        def _(sp):
            sp.dma_start(xs[:, 0:QT, :], x_v[:, 0:QT, :]).then_inc(x_first, 16)
            sp.dma_start(selraw[0:HE, :], sel_v_w).then_inc(small_in, 16)
            sp.dma_start(selraw[HE:2 * HE, :], sel_o_w).then_inc(small_in, 16)
            sp.dma_start(qraw[:], q_w.rearrange("(h p) d -> p h d", p=P)).then_inc(small_in, 16)
            sp.dma_start(kraw[:], k_w.rearrange("(h p) d -> p h d", p=P)).then_inc(small_in, 16)
            sp.dma_start(wraw[:], W_qkv.rearrange("(t p) d -> p t d", p=P)).then_inc(small_in, 16)
            sp.dma_start(woraw[:], W_out).then_inc(small_in, 16)
            sp.dma_start(braw[:], b_qkv.rearrange("(a n) -> a n", a=1)).then_inc(small_in, 16)
            sp.dma_start(bout[:], b_out.rearrange("(a n) -> a n", a=1)).then_inc(small_in, 16)
            sp.dma_start(rsraw[:], route_scale.rearrange("(a n) -> a n", a=1)).then_inc(small_in, 16)
            for n in range(2 * H):
                if n >= 4:
                    sp.wait_ge(raw_free[n % 4], n // 4)
                src = (wv_v, wo_v)[n % 2][:, (n // 2) * E:(n // 2 + 1) * E, :]
                sp.dma_start(raw[:, n % 4], src).then_inc(experts_in[n % 4], 16)
            sp.dma_start(xs[:, QT:, :], x_v[:, QT:, :]).then_inc(x_rest, 16)
            with sp.Fori(0, B) as b:
                sp.wait_ge(x_ffn, b + (B + 2))
                sp.dma_start(out_v[:, bass.ts(b, QT), :], xs[:, bass.ts(b, QT), :]).then_inc(stored, 16)
            sp.wait_ge(stored, 16 * B)

        @block.tensor
        def _(pe):
            mm, tr = nc.tensor.matmul, nc.tensor.transpose

            def split3(o, hi, lo, rhi, rlo):
                mm(o, hi, rhi, start=True, stop=False)
                mm(o, hi, rlo, start=False, stop=False)
                return mm(o, lo, rhi, start=False, stop=True)

            def prep_transpose(n):
                pe.wait_ge(xn_ready, n + 1)
                for k in range(QT):
                    last = tr(qc[:, k * P:(k + 1) * P], xn[:, k, :], ident[:])
                last.then_inc(xt_mm, 1)

            def prep_logits(n):
                pe.wait_ge(xt_ready, n + 1)
                for k in range(QT):
                    last = mm(qc[:, k * P:(k + 1) * P], xT[:, k * P:(k + 1) * P], selT[:], start=True, stop=True)
                last.then_inc(lg_mm, 1)

            pe.wait_ge(small_in, SMALL)
            pe.wait_ge(ident_set, 1)
            tr(bank[0][:, 0:P], selraw[:], ident[:])
            tr(bank[0][:, P:2 * P], woraw[:], ident[:]).then_inc(tr_small, 1)
            for t in range(3):
                last = tr(bank[1][:, t * P:(t + 1) * P], wraw[:, t, :], ident[:])
            last.then_inc(tr_small, 1)
            for h in range(H):
                last = mm(bank[2 + h // 4][:, (h % 4) * P:(h % 4 + 1) * P], qraw[:, h, :], kraw[:, h, :],
                          start=True, stop=True)
            last.then_inc(mh_mm, 1)
            pe.wait_ge(ones_set, 1)
            pe.wait_ge(setup_rows, 1)
            for c in range(2 * NG + 2):
                mm(bank[4][:, c:c + 1], brow[0:1, c, :], ones[0:1, 0:1], start=True, stop=True)
            mm(bank[5][:, 0:NH * DH], ones[0:1, :], bvrow[0:1, :], start=True, stop=True)
            mm(bank[5][:, P:P + 1], ones[0:1, :], rsraw[0:1, :], start=True, stop=True).then_inc(rows_mm, 1)
            prep_transpose(0)
            pe.wait_ge(sel_ready, 1)
            prep_logits(0)

            def ffn_steps(f, b, first, last=False):
                n = 4 * f + b
                t = 8 * f + b
                q, u = 8 * n, UNITS * n

                def query(h):
                    if h == 0:
                        pe.wait_ge(prep_done, n + 1)
                    if h >= 2 or not first:
                        pe.wait_ge(c_lo, q + h - 1)
                    if h == 3 and not last:
                        pe.wait_ge(lg_exp, n + 2)
                    elif h == 3 and f == 0:
                        pe.wait_ge(xt_ready, t + 2)
                    split3(qc[:], mh[:, 0, h, :], mh[:, 1, h, :], xhl[:, 0, :], xhl[:, 1, :]).then_inc(q_mm, 1)

                def score(h, k):
                    i = QT * h + k
                    if k == 0:
                        pe.wait_ge(q_lo, q + h + 1)
                    if i >= 2 or not first:
                        pe.wait_ge(s_exp, u + i - 1)
                    c = slice(k * P, (k + 1) * P)
                    split3(sbk[i % 2][:], qhl[:, 0, c], qhl[:, 1, c], xhl[:, 0, :], xhl[:, 1, :]).then_inc(s_mm, 1)

                def values(h, k, half):
                    i = QT * h + k
                    c = slice(k * P, (k + 1) * P)
                    done, free = ((v0_mm, v_act), (v1_mm, v_dve))[half]
                    if i >= 1 or not first:
                        pe.wait_ge(free, u + i)
                    e = slice(h * E + half * G, h * E + (half + 1) * G)
                    split3(gb[half][:], xhl[:, 0, c], xhl[:, 1, c], wv[:, 0, e, :], wv[:, 1, e, :]).then_inc(done, 1)

                def transposes(h, k):
                    i = QT * h + k
                    pe.wait_ge(s_exp, u + i + 1)
                    if i >= 1 or not first:
                        pe.wait_ge((pt_dve, pt_act)[(i - 1) % 2], 16 * n + (i - 1) // 2 + 1)
                    for c in range(QT):
                        last = tr(tb[:, c * P:(c + 1) * P], pp[:, i % 2, c * P:(c + 1) * P], ident[:])
                    last.then_inc(t_mm, 1)

                def context(h, shared):
                    pe.wait_ge(pt_act, 16 * n + 2 * h + 2)
                    pe.wait_ge(pt_dve, 16 * n + 2 * h + 2)
                    pe.wait_ge(v_fold, u + QT * (h + 1))
                    if shared:
                        pe.wait_ge(q_lo, q + h + 2)
                    for c in range(QT):
                        last = mm(qc[:], vv[:, h % 2, c, :], pt[:, c, :], start=(c == 0), stop=(c == QT - 1))
                    last.then_inc(av_mm, 1)

                def outputs(h, k, half):
                    i = QT * h + k
                    c = slice(k * P, (k + 1) * P)
                    done, free = ((o0_mm, o_act), (o1_mm, o_dve))[half]
                    if k == 0 and half == 0:
                        pe.wait_ge(c_lo, q + h + 1)
                    if i >= 1 or not first:
                        pe.wait_ge(free, u + i)
                    e = slice(h * E + half * G, h * E + (half + 1) * G)
                    split3(gb[2 + half][:], chl[:, 0, c], chl[:, 1, c], wo[:, 0, e, :], wo[:, 1, e, :]).then_inc(done, 1)

                return query, score, values, transposes, context, outputs

            def ffn_begin(f):
                query, _, values, _, _, _ = ffn_steps(f, 0, True)
                if f == 1:
                    pe.wait_ge(x_mha, B + 1)
                query(0)
                for k in range(QT):
                    values(0, k, 0)
                    values(0, k, 1)

            def ffn_stage(f, b, first, last):
                t, q = 8 * f + b, 8 * (4 * f + b)
                query, score, values, transposes, context, outputs = ffn_steps(f, b, first, last)
                if not last:
                    next_query, _, next_values, _, _, _ = ffn_steps(f, b + 1, False)
                for h in range(H - 1):
                    past = h >= 1
                    for k in range(QT):
                        values(h + 1, k, 0)
                        if past and k == 2:
                            outputs(h - 1, k, 0)
                        score(h, k)
                        if past and k == 1:
                            outputs(h - 1, k, 0)
                        if k >= 1:
                            transposes(h, k - 1)
                        if k == QT - 1:
                            query(h + 1)
                        values(h + 1, k, 1)
                        if past and k == 0:
                            outputs(h - 1, k, 0)
                        if k == QT - 1:
                            transposes(h, k)
                        if past and k == QT - 1:
                            outputs(h - 1, k, 0)
                        if past:
                            outputs(h - 1, k, 1)
                        if (h, k) == (2, 0) and not (f and last):
                            pe.wait_ge(c_lo, q + 2)
                            prep_transpose(t + 1)
                        if (h, k) == (2, 1) and not last:
                            prep_logits(t + 1)
                    context(h, True)
                score(H - 1, 0)
                for k in range(QT):
                    if k < QT - 1:
                        score(H - 1, k + 1)
                    if k >= 1:
                        transposes(H - 1, k - 1)
                    outputs(H - 2, k, 0)
                    outputs(H - 2, k, 1)
                if not last:
                    next_query(0)
                transposes(H - 1, QT - 1)
                if not last:
                    next_values(0, 0, 0)
                    next_values(0, 0, 1)
                context(H - 1, not last)
                for k in range(QT):
                    if not last and k < QT - 1:
                        next_values(0, k + 1, 0)
                        next_values(0, k + 1, 1)
                    outputs(H - 1, k, 0)
                    outputs(H - 1, k, 1)

            def mha_steps(b, first):
                t = B + b
                m = MU * b

                def free(what):
                    at = PLACE[what] - 3
                    if at < 0 and first:
                        return
                    kind, i = FLOW[at]
                    if kind == "output" and first:
                        kind, i = FLOW[at - 3]
                    if kind == "score":
                        pe.wait_ge(m_max, m + i + 1 - (MU if at < 0 else 0))
                    elif kind == "values":
                        pe.wait_ge(vext_ready, b + 1)
                    else:
                        pe.wait_ge(x_mha, b + 1)

                def stack(g, part):
                    if g == 0 and part == 0:
                        pe.wait_ge(xt_ready, t + 1)
                    if g >= 1:
                        pe.wait_ge(qk_ready, 2 * NG * b + 2 * g - 1 + part)
                    if part == 0 and g == 3 and not first:
                        pe.wait_ge(ont_ready, b)
                    elif part == 0 and not first:
                        pe.wait_ge(on_ready, NG * b + g - 3)
                    if part == 1 and (g >= 2 or not first):
                        pe.wait_ge(m_added, NG * b + g - 1)
                    mm((qc, kc)[part][:], (wqs, wks)[part][:, g, :], xT[:], start=True, stop=True).then_inc(qk_mm, 1)

                def value_product():
                    free(("values", 0))
                    o = bank[PLACE["values", 0] % 3]
                    for k in range(QT):
                        last = mm(o[:, k * P:(k + 1) * P], xT[:, k * P:(k + 1) * P], wvT[:], start=True, stop=True)
                    last.then_inc(mv_mm, 1)

                def score(i):
                    g, k, j = i // GU, i // GH % QT, i % GH
                    if i % GU == 0:
                        pe.wait_ge(qk_ready, 2 * NG * b + 2 * g + 2)
                    free(("score", i))
                    r = slice(R * j, R * j + R)
                    mm(bank[PLACE["score", i] % 3][:], qk[r, g, 0, k * P:(k + 1) * P], qk[r, g, 1, :],
                       start=True, stop=True).then_inc(ms_mm, 1)

                def maxima(g):
                    pe.wait_ge(m_split, NG * b + g + 1)
                    for k in range(QT):
                        last = tr(kc[:, k * P:(k + 1) * P],
                                  mrow[:, k, :, :].rearrange("p j r -> p (j r)").bitcast(F32), ident[:])
                    last.then_inc(m_tr, 1)

                def score_t(i):
                    g, c, j = i // GU, i // GH % QT, i % GH
                    if i % GU == 0:
                        pe.wait_ge(m_added, NG * b + g + 1)
                    if i >= 2 or not first:
                        pe.wait_ge(m_exp, m + i - 1)
                    r = slice(R * j, R * j + R)
                    mm(bank[3 + i % 2][:], qk[r, g, 1, c * P:(c + 1) * P], qk[r, g, 0, :],
                       start=True, stop=True).then_inc(mb_mm, 1)

                def context(a):
                    g, c = a // QT, a % QT
                    pe.wait_ge(m_exp, m + GH * (a + 1))
                    if c == 0 and g == 0:
                        pe.wait_ge(vext_ready, b + 1)
                    if c == 0 and (g >= 1 or not first):
                        pe.wait_ge(ot_ready, NG * b + g)
                    for j in range(GH):
                        last = mm(tb[R * j:R * j + R // 2, :], vext[:, c, GH * g + j, :],
                                  pm[:, (GH * a + j) % (2 * GH), :],
                                  start=(c == 0), stop=(c == QT - 1), skip_group_check=True)
                    last.then_inc(mav_mm, 1)

                def out_transposes(g):
                    pe.wait_ge(ot_ready, NG * b + g + 1)
                    if g >= 1 or not first:
                        pe.wait_ge(on_ready, NG * b + g)
                    for k in range(QT):
                        last = tr(qc[:, k * P:(k + 1) * P], oT[:, k * P:(k + 1) * P], ident[:])
                    last.then_inc(ott_mm, 1)

                def output_transposes():
                    pe.wait_ge(on_ready, NG * b + NG)
                    for k in range(QT):
                        last = tr(qc[:, k * P:(k + 1) * P], oN[:, k, :, :].rearrange("p h d -> p (h d)"), ident[:])
                    last.then_inc(ont_mm, 1)

                def output_product(wait):
                    wait()
                    pe.wait_ge(ont_ready, b + 1)
                    for k in range(QT):
                        o = bank[PLACE["output", 0] % 3][:, k * P:(k + 1) * P]
                        mm(o, oT[:, k * P:(k + 1) * P], woT[:], start=True, stop=False)
                        last = mm(o, ones[0:1, :], bout[0:1, :], start=False, stop=True)
                    last.then_inc(proj_mm, 1)

                return (free, stack, value_product, score, maxima, score_t, context, out_transposes,
                        output_transposes, output_product)

            def mha_finish(prev, s, alone, next_qk):
                b = prev[-1]
                _, _, _, _, maxima, score_t, context, out_transposes, output_transposes, output_product = prev[:-1]
                i = s - LAG + MU
                if i < MU:
                    score_t(i)
                if i % GH == 2 and i < MU + GH:
                    context(i // GH - 1)
                if s == 3:
                    if not alone:
                        pe.wait_ge(qk_ready, next_qk + 2)
                    maxima(NG - 1)
                if s in (0, 16, 32):
                    if alone:
                        pe.wait_ge(lg_exp, B + 1)
                    else:
                        pe.wait_ge(qk_ready, next_qk + 2 + s // 8)
                    out_transposes(1 + s // 16)
                if s == 36:
                    output_transposes()

            def mha_stage(b, first, last):
                t, m = B + b, MU * b
                steps = mha_steps(b, first)
                free, stack, value_product, score, maxima, score_t, context, out_transposes, _, _ = steps
                if not last:
                    next_stack = mha_steps(b + 1, False)[1]
                if not first:
                    prev = mha_steps(b - 1, False) + (b - 1,)
                    last_output_product = prev[-2]
                for s in range(MU):
                    g, w = s // GU, s % GU
                    i = s - LAG
                    if s == V_STEP:
                        value_product()
                    if s == PROJ_STEP and not first:
                        last_output_product(lambda: free(("output", 0)))
                    score(s)
                    if not first:
                        mha_finish(prev, s, False, 2 * NG * b)
                    if i >= 0:
                        score_t(i)
                    if i >= GH and i % GH == 2:
                        context(i // GH - 1)
                    if g < NG - 1 and w in (6, 9):
                        stack(g + 1, w // 9)
                    if g >= 1 and w == 3:
                        pe.wait_ge(qk_ready, 2 * NG * b + 2 * g + 2)
                        maxima(g - 1)
                    if s == 44:
                        pe.wait_ge(qk_ready, 2 * NG * b + 2 * NG - 1)
                        prep_transpose(t + 1)
                    if s == 48:
                        pe.wait_ge(xt_ready, t + 2)
                        out_transposes(0)
                    if s == 56 and last:
                        pe.wait_ge(on_ready, NG * b + 1)
                        prep_logits(t + 1)
                    if s in (54, 57) and not last:
                        next_stack(0, s // 57)

            ffn_begin(0)
            ffn_stage(0, 0, True, False)
            with pe.Fori(1, B - 1) as b:
                ffn_stage(0, b, False, False)
            ffn_stage(0, B - 1, False, True)
            pe.wait_ge(x_ffn, B + 1)
            first_stack = mha_steps(0, True)[1]
            for part in range(2):
                first_stack(0, part)
            mha_stage(0, True, False)
            with pe.Fori(1, B - 1) as b:
                mha_stage(b, False, False)
            mha_stage(B - 1, False, True)
            steps = mha_steps(B - 1, False)
            output_product = steps[-1]
            for s in range(TAIL):
                if s == PROJ_STEP:
                    output_product(lambda: pe.wait_ge(m_max, MU * B))
                mha_finish(steps + (B - 1,), s, True, 0)
            ffn_begin(1)
            ffn_stage(1, 0, True, False)
            with pe.Fori(1, B - 1) as b:
                ffn_stage(1, b, False, False)
            ffn_stage(1, B - 1, False, True)

        @block.scalar
        def _(act):
            activation = nc.scalar.activation

            def prep(n):
                act.wait_ge(xt_mm, n + 1)
                activation(xT[:], qc[:], ACT.Copy).then_inc(xt_ready, 1)

            def prep_exp(n):
                act.wait_ge(lg_mm, n + 1)
                activation(xn[:].rearrange("p t d -> p (t d)"), qc[:], ACT.Exp, scale=-1.0).then_inc(lg_exp, 1)

            def experts(*heads):
                for n in heads:
                    act.wait_ge(experts_in[n % 4], 16 * (n // 4 + 1))
                    w = (wv, wo)[n % 2]
                    h = n // 2
                    activation(w[:, 0, h * E:(h + 1) * E, :], raw[:, n % 4], ACT.Copy).then_inc(experts_hi, 1)

            act.wait_ge(mh_mm, 1)
            for h in range(2):
                last = activation(mf[:, 4 * h:4 * h + 4, :].rearrange("p h d -> p (h d)"), bank[2 + h][:], ACT.Copy,
                                  scale=-FFN_SCALE)
            last.then_inc(mh_scaled, 1)
            experts(0, 1, 2)
            prep(0)
            experts(3)
            prep_exp(0)
            experts(*range(4, 2 * H))

            def ffn_steps(f, b, first):
                n = 4 * f + b
                t = 8 * f + b
                q, u = 8 * n, UNITS * n

                def query(h):
                    act.wait_ge(q_mm, q + h + 1)
                    activation(qhl[:, 0, :], qc[:], ACT.Copy).then_inc(q_hi, 1)

                def context(h):
                    act.wait_ge(av_mm, q + h + 1)
                    activation(chl[:, 0, :], qc[:], ACT.Copy).then_inc(c_hi, 1)

                def values(h, k):
                    i = QT * h + k
                    act.wait_ge(v0_mm, u + i + 1)
                    if i == 0:
                        act.wait_ge(gates_in, n + 1)
                    if i >= 2 or not first:
                        act.wait_ge(v_fold, u + i - 1)
                    for e in range(G):
                        last = activation(vt[:, i % 2, e * P:(e + 1) * P], gb[0][:, e * P:(e + 1) * P], ACT.Copy,
                                          scale=gate[:, k, h * E + e:h * E + e + 1])
                    last.then_inc(v_act, 1)

                def softmax(h, k):
                    i = QT * h + k
                    act.wait_ge(s_min, u + i + 1)
                    if i >= 2 or not first:
                        act.wait_ge(t_mm, u + i - 1)
                    activation(pp[:, i % 2, :], sbk[i % 2][:], ACT.Exp, bias=nmin[:, h % 2, k:k + 1], scale=-1.0,
                               accum_out=den[:, h % 2, k:k + 1]).then_inc(s_exp, 1)

                def copy_pt(h, k):
                    i = QT * h + k
                    act.wait_ge(t_mm, u + i + 1)
                    if k == 1 and (h >= 1 or not first):
                        act.wait_ge(av_mm, q + h)
                    activation(pt[:, :, k * P:(k + 1) * P], tb[:].rearrange("p (c q) -> p c q", c=QT),
                               ACT.Copy).then_inc(pt_act, 1)

                def outputs(h, k):
                    i = QT * h + k
                    act.wait_ge(o0_mm, u + i + 1)
                    if k == 0:
                        act.wait_ge(gn_ready, q + h + 1)
                    if i == 0:
                        act.wait_ge(x_ffn, n + 1)
                    if h >= 1 and i - QT >= 2:
                        act.wait_ge(o_acc, (UNITS - QT) * n + i - QT - 1)
                    o = acc[:, k, :] if h == 0 else ot[:, i % 2, :]
                    for e in range(G):
                        last = activation(o[:, e * D:(e + 1) * D], gb[2][:, e * D:(e + 1) * D], ACT.Copy,
                                          scale=gn[:, h % 2, k, e:e + 1])
                    last.then_inc(o_act, 1)

                return query, context, values, softmax, copy_pt, outputs

            def ffn_begin(f):
                query, _, values, _, _, _ = ffn_steps(f, 0, True)
                if f == 1:
                    act.wait_ge(x_mha, B + 1)
                query(0)
                for k in range(QT):
                    values(0, k)

            def ffn_stage(f, b, first, last):
                n, t = 4 * f + b, 8 * f + b
                query, context, values, softmax, copy_pt, outputs = ffn_steps(f, b, first)
                if not last:
                    next_query, _, next_values, _, _, _ = ffn_steps(f, b + 1, False)
                for h in range(H - 1):
                    past = h >= 1
                    for k in range(QT):
                        values(h + 1, k)
                        if past and k in (1, 2):
                            outputs(h - 1, k)
                        softmax(h, k)
                        if k == QT - 1:
                            query(h + 1)
                            copy_pt(h, k)
                        if past and k in (0, 3):
                            outputs(h - 1, k)
                        if k == 2:
                            copy_pt(h, 1)
                        if (h, k) == (2, 0) and not (f and last):
                            prep(t + 1)
                        if (h, k) == (2, 2) and not last:
                            prep_exp(n + 1)
                    context(h)
                softmax(H - 1, 0)
                for k in range(QT):
                    if k == 2:
                        softmax(H - 1, k + 1)
                        copy_pt(H - 1, 1)
                    outputs(H - 2, k)
                    if k < 2:
                        softmax(H - 1, k + 1)
                if not last:
                    next_query(0)
                copy_pt(H - 1, QT - 1)
                if not last:
                    next_values(0, 0)
                context(H - 1)
                for k in range(QT):
                    if not last and k < QT - 1:
                        next_values(0, k + 1)
                    outputs(H - 1, k)

            def mha_steps(b, first):
                m = MU * b

                def stack(g, c):
                    if not first:
                        act.wait_ge(mb_mm, m - MU + GU * (g + 1))
                    act.wait_ge(qk_mm, 2 * NG * b + 2 * g + c + 1)
                    activation(qk[:, g, c, :], (qc, kc)[c][:], ACT.Identity,
                               bias=bst[:, c * NG + g:c * NG + g + 1]).then_inc(qk_hi, 1)

                def softmax(i):
                    act.wait_ge(mb_mm, m + i + 1)
                    if i >= 2 * GH or not first:
                        act.wait_ge(mav_mm, QT * NG * b + i // GH - 1)
                    activation(pm[:, i % (2 * GH), :], bank[3 + i % 2][:], ACT.Exp).then_inc(m_exp, 1)

                def copy_out(g):
                    act.wait_ge(mav_mm, QT * NG * b + QT * (g + 1))
                    if g >= 1:
                        act.wait_ge(ott_mm, NG * b + g)
                    elif not first:
                        act.wait_ge(proj_mm, b)
                    activation(oT[:], tb[:], ACT.Copy).then_inc(ot_ready, 1)

                def copy_output():
                    act.wait_ge(ont_mm, b + 1)
                    activation(oT[:], qc[:], ACT.Copy).then_inc(ont_ready, 1)

                return stack, softmax, copy_out, copy_output

            def mha_finish(prev, s):
                _, softmax, copy_out, copy_output = prev
                if s < LAG:
                    softmax(MU + s - LAG)
                if s in (14, 30):
                    copy_out(2 + s // 16)
                if s == 37:
                    copy_output()

            def mha_stage(b, first, last):
                t = B + b
                stack, softmax, copy_out, _ = mha_steps(b, first)
                for s in range(MU):
                    g, w = s // GU, s % GU
                    if not first:
                        mha_finish(mha_steps(b - 1, False), s)
                    if s >= LAG:
                        softmax(s - LAG)
                    if g < NG - 1 and w in (7, 10):
                        stack(g + 1, w // 10)
                    if s in (46, 62):
                        copy_out(s // 16 - 2)
                    if s == 45:
                        prep(t + 1)
                    if s == 57 and last:
                        prep_exp(B)
                    if s in (55, 58) and not last:
                        mha_steps(b + 1, False)[0](0, s // 58)

            ffn_begin(0)
            ffn_stage(0, 0, True, False)
            with act.Fori(1, B - 1) as b:
                ffn_stage(0, b, False, False)
            ffn_stage(0, B - 1, False, True)
            act.wait_ge(x_ffn, B + 1)
            for c in range(2):
                mha_steps(0, True)[0](0, c)
            mha_stage(0, True, False)
            with act.Fori(1, B - 1) as b:
                mha_stage(b, False, False)
            mha_stage(B - 1, False, True)
            for s in range(TAIL):
                mha_finish(mha_steps(B - 1, False), s)
            ffn_begin(1)
            ffn_stage(1, 0, True, False)
            with act.Fori(1, B - 1) as b:
                ffn_stage(1, b, False, False)
            ffn_stage(1, B - 1, False, True)

        @block.vector
        def _(dve):
            v = nc.vector
            own = Chain(dve, dve_own)
            PREP = 10 + 3 * (E - 1)
            FFN_OWN = PREP + H
            MHA_OWN = 2 * NG + 1
            M = QT * 2 * H
            pr = xn[:].rearrange("p t (g e) -> p (t g) e", e=E)

            def tile_statistics(nb, k):
                return v.bn_stats(st[:, k, :], xs[:, nb * QT + k, :])

            def statistics(nb, done=0):
                for k in range(done, QT):
                    last = tile_statistics(nb, k)
                own.link(last)
                v.memset(tick[:], 0.0)
                for k in range(QT):
                    last = v.bn_aggr(mv[:, k, :], st[:, k, :])
                last.then_inc(mv_ready, 1)

            def normalise(n, nb, tiles=range(QT)):
                for k in tiles:
                    if k == 0:
                        dve.wait_ge(rstd_ready, n + 1)
                    last = v.tensor_scalar(xn[:, k, :], xs[:, nb * QT + k, :], mv[:, k, 0:1], rstd[:, k:k + 1],
                                           ALU.subtract, ALU.mult)
                    if k == QT - 1:
                        last.then_inc(xn_ready, 1)

            def denominators(n):
                dve.wait_ge(lg_exp, n + 1)
                own.link(v.memset(cnt[:], 0.0))
                own.link(v.tensor_scalar_add(pr, pr, 1.0))

            def sigmoids(half):
                o = xn[:, half * QT // 2:(half + 1) * QT // 2, :]
                own.link(v.reciprocal(o, o))

            def ranks(*distances):
                for k in distances:
                    own.link(v.tensor_tensor(cmp_[:, :, 0:E - k], pr[:, :, 0:E - k], pr[:, :, k:E], ALU.is_ge))
                    own.link(v.tensor_tensor(cnt[:, :, k:E], cnt[:, :, k:E], cmp_[:, :, 0:E - k], ALU.add))
                    own.link(v.tensor_tensor(cnt[:, :, 0:E - k], cnt[:, :, 0:E - k], cmp_[:, :, 0:E - k], ALU.subtract))

            def mask_best():
                v.tensor_tensor(cmp_[:], cnt[:], thr[:].unsqueeze(1).to_broadcast([P, M, E]), ALU.is_lt)\
                    .then_inc(best_masked, 1)

            def over_sum(n):
                dve.wait_ge(best_picked, n + 1)
                own.link(v.tensor_reduce(gsum[:], pr, AX.X, ALU.add))
                own.link(v.tensor_scalar_max(gsum[:], gsum[:], 1e-9))
                own.link(v.reciprocal(gsum[:], gsum[:]))
                own.link(v.tensor_tensor(gsum[:].rearrange("p (t g) -> p t g", t=QT),
                                         gsum[:].rearrange("p (t g) -> p t g", t=QT),
                                         rsb[:].unsqueeze(1).to_broadcast([P, QT, 2 * H]), ALU.mult))

            def weights():
                v.tensor_tensor(gate[:].rearrange("p t (g e) -> p (t g) e", e=E), pr,
                                gsum[:].unsqueeze(2).to_broadcast([P, M, E]), ALU.mult).then_inc(gates_in, 1)

            def gates(n):
                denominators(n)
                sigmoids(0)
                sigmoids(1)
                ranks(*range(1, E))
                mask_best()
                over_sum(n)
                weights()

            def commit_x():
                own.link(v.tensor_copy(xhl[:, 0, :], xT[:]))
                v.tensor_tensor(xhl[:, 1, :], xT[:], xhl[:, 0, :].bitcast(F32), ALU.subtract).then_inc(prep_done, 1)

            v.memset(ones[:], 1.0)
            v.memset(ph[:], -0.5)
            v.memset(eps[:], LN_EPS)
            v.memset(wqs[:], 0.0)
            v.memset(wks[:], 0.0)
            for e in range(E):
                v.memset(thr[:, e:e + 1], float(e - (E - 3)))
            own.link(v.memset(brow[:], 0.0))
            v.tensor_copy(ones[:], ones[:]).then_inc(ones_set, 1)
            v.memset(gsum[:], 0.0).then_inc(x_mha, 1)
            dve.wait_ge(x_first, 16)
            statistics(0)
            normalise(0, 0)
            dve.wait_ge(small_in, SMALL)
            heads = braw[:].rearrange("p (h c) -> p h c", h=NH)
            for r in range(3):
                c = slice(DH * r, DH * r + DH)
                v.tensor_scalar_mul(brow[0:1, 0:NG, :].rearrange("p g (j r) -> p (g j) r", j=GH)[:, :, c],
                                    heads[:, :, 0:DH], MHA_SCALE)
                v.tensor_copy(brow[0:1, NG:2 * NG, :].rearrange("p g (j r) -> p (g j) r", j=GH)[:, :, c],
                              heads[:, :, DH:2 * DH])
            v.memset(brow[0:1, NG:2 * NG, :].rearrange("p g (j r) -> p (g j) r", j=GH)[:, :, 3 * DH:3 * DH + 2], -1.0)
            v.memset(brow[0:1, 2 * NG, :].rearrange("p (j r) -> p j r", j=GH)[:, :, 2 * DH:3 * DH], -1.0)
            v.memset(brow[0:1, 2 * NG + 1, :].rearrange("p (j r) -> p j r", j=GH)[:, :, DH:2 * DH], -1.0)
            v.tensor_copy(bvrow[:].rearrange("p (h c) -> p h c", h=NH), heads[:, :, 2 * DH:3 * DH])\
                .then_inc(setup_rows, 1)
            dve.wait_ge(tr_small, 2)
            v.tensor_copy(selT[:], bank[0][:, 0:P]).then_inc(sel_ready, 1)
            v.tensor_copy(woT[:], bank[0][:, P:2 * P])
            wh = bank[1][:, 0:3 * P].rearrange("p (h c) -> p h c", h=NH)
            for r in range(3):
                c = slice(DH * r, DH * r + DH)
                v.tensor_scalar_mul(wqs[:].rearrange("p g (j r) -> p (g j) r", j=GH)[:, :, c], wh[:, :, 0:DH], MHA_SCALE)
                v.tensor_copy(wks[:].rearrange("p g (j r) -> p (g j) r", j=GH)[:, :, c], wh[:, :, DH:2 * DH])
            v.tensor_copy(wvT[:].rearrange("p (h c) -> p h c", h=NH), wh[:, :, 2 * DH:3 * DH])
            dve.wait_ge(rows_mm, 1)
            v.tensor_copy(bst[:], bank[4][:, 0:2 * NG + 2])
            v.tensor_copy(bvb[:], bank[5][:, 0:NH * DH])
            v.tensor_copy(rsb[:, 0:H], bank[5][:, P:P + 1].to_broadcast([P, H]))
            own.link(v.tensor_scalar_mul(rsb[:, H:2 * H], bank[5][:, P:P + 1].to_broadcast([P, H]), 0.5))
            dve.wait_ge(mh_scaled, 1)
            own.link(v.tensor_copy(mh[:, 0, :, :], mf[:]))
            v.tensor_tensor(mh[:, 1, :, :], mf[:], mh[:, 0, :, :].bitcast(F32), ALU.subtract)

            def experts(*heads):
                for h in heads:
                    dve.wait_ge(experts_hi, 2 * h + 1)
                    v.tensor_tensor(wv[:, 1, h * E:(h + 1) * E, :], raw[:, 2 * h % 4],
                                    wv[:, 0, h * E:(h + 1) * E, :].bitcast(F32), ALU.subtract)\
                        .then_inc(raw_free[2 * h % 4], 1)

            experts(0, 1)
            denominators(0)
            sigmoids(0)
            experts(2)
            sigmoids(1)
            experts(3)
            ranks(1, 2)
            experts(4)
            ranks(3, 4)
            experts(5)
            ranks(5, 6, 7)
            experts(6)
            mask_best()
            over_sum(0)
            weights()
            experts(7)
            commit_x()
            dve.wait_ge(x_rest, 16)

            def ffn_steps(f, b, first):
                n = 4 * f + b
                t = 8 * f + b
                q, u = 8 * n, UNITS * n
                nb = (b + 1) % B

                def query(h):
                    dve.wait_ge(q_hi, q + h + 1)
                    v.tensor_tensor(qhl[:, 1, :], qc[:], qhl[:, 0, :].bitcast(F32), ALU.subtract).then_inc(q_lo, 1)

                def context(h):
                    dve.wait_ge(c_hi, q + h + 1)
                    v.tensor_tensor(chl[:, 1, :], qc[:], chl[:, 0, :].bitcast(F32), ALU.subtract).then_inc(c_lo, 1)

                def row_max(h, k):
                    i = QT * h + k
                    dve.wait_ge(s_mm, u + i + 1)
                    v.tensor_reduce(nmin[:, h % 2, k:k + 1], sbk[i % 2][:], AX.X, ALU.min).then_inc(s_min, 1)

                def values(h, k):
                    i = QT * h + k
                    dve.wait_ge(v1_mm, u + i + 1)
                    dve.wait_ge(v_act, u + i + 1)
                    for e in range(G):
                        o = vt[:, i % 2, e * P:(e + 1) * P]
                        last = v.scalar_tensor_tensor(o, gb[1][:, e * P:(e + 1) * P],
                                                      gate[:, k, h * E + G + e:h * E + G + e + 1], o, ALU.mult, ALU.add)
                    last.then_inc(v_dve, 1)

                def outputs(h, k):
                    i = QT * h + k
                    dve.wait_ge(o1_mm, u + i + 1)
                    dve.wait_ge(o_act, u + i + 1)
                    if k == 0:
                        dve.wait_ge(gn_ready, q + h + 1)
                    row = acc[:, k, :] if h == 0 else ot[:, i % 2, :]
                    for e in range(G):
                        o = row[:, e * D:(e + 1) * D]
                        last = v.scalar_tensor_tensor(o, gb[3][:, e * D:(e + 1) * D],
                                                      gn[:, h % 2, k, G + e:G + e + 1], o, ALU.mult, ALU.add)
                    last.then_inc(o_dve, 1)

                def copy_pt(h, k):
                    i = QT * h + k
                    dve.wait_ge(t_mm, u + i + 1)
                    if k == 0 and (h >= 1 or not first):
                        dve.wait_ge(av_mm, q + h)
                    v.tensor_copy(pt[:, :, k * P:(k + 1) * P], tb[:].rearrange("p (c q) -> p c q", c=QT))\
                        .then_inc(pt_dve, 1)

                def output_gates(h):
                    dve.wait_ge(s_exp, u + QT * (h + 1))
                    own.link(v.reciprocal(rden[:, h % 2, :], den[:, h % 2, :]))
                    v.tensor_tensor(gn[:, h % 2, :, :], gate[:, :, HE + h * E:HE + (h + 1) * E],
                                             rden[:, h % 2, :].unsqueeze(2).to_broadcast([P, QT, E]), ALU.mult)\
                        .then_inc(gn_ready, 1)

                return query, context, row_max, values, outputs, copy_pt, output_gates

            def ffn_begin(f):
                query, _, _, values, _, _, _ = ffn_steps(f, 0, True)
                query(0)
                for k in range(QT):
                    values(0, k)

            def ffn_stage(f, b, first, last):
                n, t = 4 * f + b, 8 * f + b
                q, nb = 8 * n, (b + 1) % B
                query, context, row_max, values, outputs, copy_pt, output_gates = ffn_steps(f, b, first)
                if not last:
                    next_query, _, _, next_values, _, _, _ = ffn_steps(f, b + 1, False)
                for h in range(H - 1):
                    for k in range(QT):
                        row_max(h, k)
                        if k % 2 == 1:
                            copy_pt(h, k - 1)
                        if k == QT - 1:
                            query(h + 1)
                        values(h + 1, k)
                        if h >= 1:
                            outputs(h - 1, k)
                        if (h, k) == (1, 2) and not (f and last):
                            dve.wait_ge(x_ffn, n + 1)
                            statistics(nb)
                    output_gates(h)
                    if h == 1 and not (f and last):
                        normalise(t + 1, nb)
                    if h == 2 and not last:
                        denominators(n + 1)
                    if h in (2, 3) and not last:
                        sigmoids(h - 2)
                    if h in (3, 4, 5, 6) and not last:
                        ranks(*((7,), (1, 2), (3, 4), (5, 6))[h - 3])
                    if h == H - 2 and not last:
                        mask_best()
                    context(h)
                row_max(H - 1, 0)
                for k in range(QT):
                    if k < QT - 1:
                        row_max(H - 1, k + 1)
                    if k == 2 and not last:
                        commit_x()
                    if k % 2 == 1:
                        copy_pt(H - 1, k - 1)
                    outputs(H - 2, k)
                    if k == 2 and not last:
                        over_sum(n + 1)
                if not last:
                    next_query(0)
                output_gates(H - 1)
                if not last:
                    dve.wait_ge(gn_ready, q + H)
                    weights()
                if not last:
                    next_values(0, 0)
                context(H - 1)
                for k in range(QT):
                    if not last and k < QT - 1:
                        next_values(0, k + 1)
                    outputs(H - 1, k)

            def mha_steps(b, first):
                m = MU * b

                def stack(g, c):
                    dve.wait_ge(qk_masked, 2 * NG * b + 2 * g + c + 1)
                    o = qk[:, g, c, :]
                    v.scalar_tensor_tensor(o, (qc, kc)[c][:], bst[:, c * NG + g:c * NG + g + 1], o.bitcast(F32),
                                           ALU.add, ALU.add).then_inc(qk_ready, 1)

                def values():
                    dve.wait_ge(mv_mm, b + 1)
                    if not first:
                        dve.wait_ge(mav_mm, QT * NG * b)
                    o = bank[PLACE["values", 0] % 3][:].rearrange("p (k h c) -> p k h c", k=QT, h=NH)
                    v.tensor_tensor(vext[:, :, :, 0:DH], o,
                                    bvb[:].rearrange("p (h c) -> p h c", h=NH).unsqueeze(1).to_broadcast([P, QT, NH, DH]),
                                    ALU.add).then_inc(vext_ready, 1)

                def row_max(i):
                    dve.wait_ge(ms_mm, m + i + 1)
                    if i % GU == 0 and (i >= 2 * GU or not first):
                        dve.wait_ge(m_split, NG * b + i // GU - 1)
                    v.tensor_reduce(mmax[:, i // GU % 2, i // GH % QT, i % GH:i % GH + 1],
                                    bank[PLACE["score", i] % 3][:], AX.X, ALU.max).then_inc(m_max, 1)

                def split_maxima(g):
                    dve.wait_ge(m_max, m + GU * (g + 1))
                    own.link(v.tensor_copy(mrow[:, :, :, 3 * DH], mmax[:, g % 2, :, :]))
                    v.tensor_tensor(mrow[:, :, :, 3 * DH + 1], mmax[:, g % 2, :, :],
                                    mrow[:, :, :, 3 * DH].bitcast(F32), ALU.subtract).then_inc(m_split, 1)

                def add_maxima(g):
                    dve.wait_ge(m_tr, NG * b + g + 1)
                    o = qk[:, g, 0, :]
                    v.tensor_tensor(o, o.bitcast(F32), kc[:], ALU.add).then_inc(m_added, 1)

                def over_sums(g):
                    dve.wait_ge(ott_mm, NG * b + g + 1)
                    if g == 0 and not first:
                        dve.wait_ge(ont_mm, b)
                    o = qc[:].rearrange("p (k j r) -> p k j r", k=QT, j=GH)
                    own.link(v.reciprocal(mrd[:], o[:, :, :, DH]))
                    v.tensor_tensor(oN[:, :, GH * g:GH * g + GH, :], o[:, :, :, 0:DH],
                                    mrd[:].unsqueeze(3).to_broadcast([P, QT, GH, DH]), ALU.mult).then_inc(on_ready, 1)

                def residual():
                    dve.wait_ge(proj_mm, b + 1)
                    xb = xs[:, bass.ts(b, QT), :]
                    o = bank[PLACE["output", 0] % 3][:].rearrange("p (k d) -> p k d", k=QT)
                    v.tensor_tensor(xb, xb, o, ALU.add).then_inc(x_mha, 1)

                return stack, values, row_max, split_maxima, add_maxima, over_sums, residual

            def mha_finish(prev, s):
                _, _, _, _, add_maxima, over_sums, residual = prev
                if s == 4:
                    add_maxima(NG - 1)
                if s in (2, 18, 34):
                    over_sums(1 + s // 16)
                if s == PROJ_STEP:
                    residual()

            def mha_stage(b, first, last):
                t, nb = B + b, (b + 1) % B
                stack, values, row_max, split_maxima, add_maxima, over_sums, _ = mha_steps(b, first)
                for s in range(MU):
                    g, w = s // GU, s % GU
                    if not first:
                        mha_finish(mha_steps(b - 1, False), s)
                    if s == V_STEP:
                        values()
                    row_max(s)
                    if g < NG - 1 and w in (9, 12):
                        stack(g + 1, w // 12)
                    if w == GU - 1:
                        if first and g == 0:
                            dve.wait_ge(mrow_set, 1)
                        split_maxima(g)
                    if g >= 1 and w == 4:
                        add_maxima(g - 1)
                    if s == 50:
                        over_sums(0)
                    if s == 5 and last:
                        dve.wait_ge(x_mha, 2)
                    if s in (5, 6, 7):
                        tile_statistics(nb, s - 5)
                    if s == 8:
                        statistics(nb, 3)
                    if s == 30:
                        if first:
                            dve.wait_ge(gates_in, B)
                        dve.wait_ge(xt_ready, t + 1)
                    if s in (30, 31, 33, 35):
                        normalise(t + 1, nb, [(s - 29) // 2])
                    if s in (57, 60) and not last:
                        mha_steps(b + 1, False)[0](0, s // 60)

            ffn_begin(0)
            ffn_stage(0, 0, True, False)
            with dve.Fori(1, B - 1) as b:
                own.enter(b - 1, FFN_OWN)
                ffn_stage(0, b, False, False)
            own.leave(B - 2)
            ffn_stage(0, B - 1, False, True)
            dve.wait_ge(x_ffn, B + 1)
            own.link(v.memset(vext[:, :, :, DH:DH + 1], 1.0))
            own.link(v.memset(vext[:, :, :, DH + 1:], 0.0))
            for c in range(2):
                mha_steps(0, True)[0](0, c)
            mha_stage(0, True, False)
            with dve.Fori(1, B - 1) as b:
                own.enter(b - 1, MHA_OWN)
                mha_stage(b, False, False)
            own.leave(B - 2)
            mha_stage(B - 1, False, True)
            for s in range(TAIL):
                mha_finish(mha_steps(B - 1, False), s)
                if s == 5:
                    gates(B)
            commit_x()
            ffn_begin(1)
            ffn_stage(1, 0, True, False)
            with dve.Fori(1, B - 1) as b:
                own.enter(b - 1, FFN_OWN)
                ffn_stage(1, b, False, False)
            own.leave(B - 2)
            ffn_stage(1, B - 1, False, True)

        @block.gpsimd
        def _(pool):
            g_ = nc.gpsimd
            own = Chain(pool, pool_own)
            PREP = 1

            def rstd_(n):
                pool.wait_ge(mv_ready, n + 1)
                own.link(g_.tensor_tensor(ve[:], mv[:, :, 1], eps[:], ALU.add))
                g_.tensor_tensor(rstd[:], ve[:], ph[:], ALU.pow).then_inc(rstd_ready, 1)

            def pick_best(n):
                pool.wait_ge(best_masked, n + 1)
                flat = xn[:].rearrange("p t d -> p (t d)")
                g_.tensor_tensor(flat, flat, cmp_[:].rearrange("p m e -> p (m e)"), ALU.mult).then_inc(best_picked, 1)

            own.link(g_.memset(ident[:], 0.0))
            g_.affine_select(out=ident[:], in_=ident[:], compare_op=ALU.not_equal, fill=1.0, base=0,
                             pattern=[[-1, P]], channel_multiplier=1).then_inc(ident_set, 1)
            g_.memset(ptick[:], 0.0).then_inc(x_ffn, 1)
            pool.wait_ge(ones_set, 1)
            rstd_(0)
            for h in range(H):
                if h == H - 1:
                    pick_best(0)
                pool.wait_ge(experts_hi, 2 * h + 2)
                g_.tensor_tensor(wo[:, 1, h * E:(h + 1) * E, :], raw[:, (2 * h + 1) % 4],
                                 wo[:, 0, h * E:(h + 1) * E, :].bitcast(F32), ALU.subtract)\
                    .then_inc(raw_free[(2 * h + 1) % 4], 1)

            def ffn_steps(f, b, first):
                n = 4 * f + b
                u = UNITS * n

                def fold_values(h, k):
                    i = QT * h + k
                    pool.wait_ge(v_dve, u + i + 1)
                    a = vt[:, i % 2, :]
                    own.link(g_.tensor_tensor(a[:, 0:2 * P], a[:, 0:2 * P], a[:, 2 * P:4 * P], ALU.add))
                    if k == 0 and (h >= 2 or not first):
                        pool.wait_ge(av_mm, 8 * n + h - 1)
                    g_.tensor_tensor(vv[:, h % 2, k, :], a[:, 0:P], a[:, P:2 * P], ALU.add).then_inc(v_fold, 1)

                def add_outputs(h, k):
                    i = QT * h + k
                    pool.wait_ge(o_dve, u + i + 1)
                    g_.tensor_tensor(acc[:, k, :], acc[:, k, :], ot[:, i % 2, :], ALU.add).then_inc(o_acc, 1)

                return fold_values, add_outputs

            def ffn_begin(f):
                fold_values, _ = ffn_steps(f, 0, True)
                for k in range(QT):
                    fold_values(0, k)

            def fold_outputs(f, b):
                pool.wait_ge(o_acc, (UNITS - QT) * (4 * f + b + 1))
                own.link(g_.tensor_tensor(acc[:, :, 0:2 * D], acc[:, :, 0:2 * D], acc[:, :, 2 * D:4 * D], ALU.add))
                own.link(g_.tensor_tensor(acc[:, :, 0:D], acc[:, :, 0:D], acc[:, :, D:2 * D], ALU.add))
                xb = xs[:, bass.ts(b, QT), :]
                g_.tensor_tensor(xb, xb, acc[:, :, 0:D], ALU.add).then_inc(x_ffn, 1)

            def ffn_stage(f, b, first, last):
                t = 8 * f + b
                fold_values, add_outputs = ffn_steps(f, b, first)
                if not last:
                    next_fold, _ = ffn_steps(f, b + 1, False)
                for h in range(H):
                    if h == H - 1 and not last:
                        pick_best(4 * f + b + 1)
                    for k in range(QT):
                        if h < H - 1:
                            fold_values(h + 1, k)
                        if h >= 2:
                            add_outputs(h - 1, k)
                    if h == 0 and not first:
                        fold_outputs(f, b - 1)
                    if h == 1 and not (f and last):
                        rstd_(t + 1)
                if not last:
                    next_fold(0, 0)
                for k in range(QT):
                    if not last and k < QT - 1:
                        next_fold(0, k + 1)
                    add_outputs(H - 1, k)
                if last:
                    fold_outputs(f, b)

            FFN_OWN = UNITS + PREP + 2
            ffn_begin(0)
            ffn_stage(0, 0, True, False)
            with pool.Fori(1, B - 1) as b:
                own.enter(b - 1, FFN_OWN)
                ffn_stage(0, b, False, False)
            own.leave(B - 2)
            ffn_stage(0, B - 1, False, True)
            pool.wait_ge(x_ffn, B + 1)
            g_.memset(mrow[:].bitcast(F32), 0.0).then_inc(mrow_set, 1)

            def mask(b, g):
                for c in range(2):
                    pool.wait_ge(qk_hi, 2 * NG * b + 2 * g + c + 1)
                    o = qk[:, g, c, :]
                    g_.tensor_tensor(o, o.bitcast(F32), bst[:, 2 * NG + c:2 * NG + c + 1].to_broadcast([P, S]),
                                     ALU.mult).then_inc(qk_masked, 1)

            def mha_stage(b, last):
                mask(b, 1)
                rstd_(B + b + 1)
                mask(b, 2)
                mask(b, 3)
                if not last:
                    mask(b + 1, 0)

            mask(0, 0)
            mha_stage(0, False)
            with pool.Fori(1, B - 1) as b:
                own.enter(b - 1, PREP)
                mha_stage(b, False)
            own.leave(B - 2)
            mha_stage(B - 1, True)
            pick_best(B)
            ffn_begin(1)
            ffn_stage(1, 0, True, False)
            with pool.Fori(1, B - 1) as b:
                own.enter(b - 1, FFN_OWN)
                ffn_stage(1, b, False, False)
            own.leave(B - 2)
            ffn_stage(1, B - 1, False, True)


_INS = ["L0_attn_x", "L0_attn_W_qkv", "L0_attn_b_qkv", "L0_attn_W_out", "L0_attn_b_out", "L0_ffn_q_w", "L0_ffn_k_w",
        "L0_ffn_v_w", "L0_ffn_o_w", "L0_ffn_sel_v_w", "L0_ffn_sel_o_w", "L0_ffn_route_scale"]


def kernel(**inputs):
    import concourse.bacc as bacc
    from concourse.bass_utils import run_bass_kernel_spmd

    nc = bacc.Bacc("TRN2", target_bir_lowering=False, num_devices=1)
    arrays, args = {}, []
    for name in _INS:
        a = np.ascontiguousarray(inputs[name])
        arrays[f"in_{name}"] = a
        args.append(nc.dram_tensor(f"in_{name}", a.shape, mybir.dt.from_np(a.dtype), kind="ExternalInput").ap())
    out = nc.dram_tensor("out_x", (B, S, D), F32, kind="ExternalOutput").ap()
    macaron_kernel(nc, *args, out)
    r = run_bass_kernel_spmd(nc, [arrays], core_ids=[0])
    return r.results[0]["out_x"]
```
